# Optimizing a Trainium2 kernel written in Bass

```python
import numpy as np
import jax
import jax.numpy as jnp

def _softmax(x, axis=-1):
    return jax.nn.softmax(x, axis=axis)

def _gelu(x):
    return jax.nn.gelu(x, approximate=True)

def _silu(x):
    return jax.nn.silu(x)

def _sigmoid(x):
    return jax.nn.sigmoid(x)

def _layernorm(x, axis=-1, eps=1e-05):
    m = jnp.mean(x, axis=axis, keepdims=True)
    v = jnp.var(x, axis=axis, keepdims=True)
    return (x - m) / jnp.sqrt(v + eps)

def _scatter_add(tgt, idx, src, axis=0):
    return tgt.at[idx].add(src)

def _segment_sum(src, seg, n):
    return jax.ops.segment_sum(src, seg, n)
kernel_name = 'mk_seq_postln_d1_jaxref_r8_f4a712'

def setup_inputs(seed: int=0):
    np.random.seed(seed)
    _w = jnp.asarray

    def _L0_attn_setup():
        import jax, jax.numpy as jnp
        import numpy as np
        B, T, DM = (2, 256, 128)
        DH = 128
        NH = DM // DH
        ROTARY_BASE = 10000.0

        def fractional_rope(x, base):
            dh = x.shape[-1]
            rot, skip = jnp.split(x, 2, axis=-1)
            width = rot.shape[-1]
            half = width // 2
            t = rot.shape[-2]
            positions = jnp.arange(t)[:, None]
            dims = jnp.arange(half)
            ang_freqs = jnp.power(base, -dims / half)[None, :]
            radians = positions * ang_freqs
            cos = jnp.cos(radians).astype(x.dtype)
            sin = jnp.sin(radians).astype(x.dtype)
            even, odd = jnp.split(rot, 2, axis=-1)
            r_even = even * cos - odd * sin
            r_odd = even * sin + odd * cos
            return jnp.concatenate([r_even, r_odd, skip], axis=-1)
        key = jax.random.key(seed)
        ks = jax.random.split(key, 5)
        scale = (1.0 / DM) ** 0.5
        x = jax.random.normal(ks[0], (B, T, DM), dtype=jnp.float32)
        wq = jax.random.normal(ks[1], (NH, DM, DH), dtype=jnp.float32) * scale
        wk = jax.random.normal(ks[2], (NH, DM, DH), dtype=jnp.float32) * scale
        wv = jax.random.normal(ks[3], (NH, DM, DH), dtype=jnp.float32) * scale
        wo = jax.random.normal(ks[4], (NH * DH, DM), dtype=jnp.float32) * (1.0 / (NH * DH)) ** 0.5
        return {'x': x, 'wq': wq, 'wk': wk, 'wv': wv, 'wo': wo}
    _L0_attn_in = _L0_attn_setup()

    def _L0_ffn_setup():
        import jax, jax.numpy as jnp
        import numpy as np

        def _binarize(w):
            alpha = jax.lax.stop_gradient(jnp.mean(jnp.abs(w), axis=1, keepdims=True))
            bw = alpha * jnp.sign(w)
            return w + jax.lax.stop_gradient(bw - w)
        key = jax.random.key(seed)
        k1, k2, k3, k4, k5 = jax.random.split(key, 5)
        D, H = (128, 512)
        x = jax.random.normal(k1, (64, 196, D), dtype=jnp.float32)
        w1 = jax.random.normal(k2, (H, D), dtype=jnp.float32) * 0.02
        b1 = jax.random.normal(k3, (H,), dtype=jnp.float32) * 0.02
        w2 = jax.random.normal(k4, (D, H), dtype=jnp.float32) * 0.02
        b2 = jax.random.normal(k5, (D,), dtype=jnp.float32) * 0.02
        return {'x': x, 'w1': w1, 'b1': b1, 'w2': w2, 'b2': b2}
    _L0_ffn_in = _L0_ffn_setup()
    _d = {'L0_attn_x': _L0_attn_in['x'], 'L0_attn_wq': _L0_attn_in['wq'], 'L0_attn_wk': _L0_attn_in['wk'], 'L0_attn_wv': _L0_attn_in['wv'], 'L0_attn_wo': _L0_attn_in['wo'], 'L0_ffn_w1': _L0_ffn_in['w1'], 'L0_ffn_b1': _L0_ffn_in['b1'], 'L0_ffn_w2': _L0_ffn_in['w2'], 'L0_ffn_b2': _L0_ffn_in['b2']}
    _x0 = _d['L0_attn_x']
    _d['L0_attn_x'] = jax.random.normal(jax.random.fold_in(jax.random.key(seed), 1), (8, 1024, 128), dtype=_x0.dtype)
    del _x0
    return _d

def reference(L0_attn_x, L0_attn_wq, L0_attn_wk, L0_attn_wv, L0_attn_wo, L0_ffn_w1, L0_ffn_b1, L0_ffn_w2, L0_ffn_b2):

    def _L0_attn_ref(x, wq, wk, wv, wo):
        import jax, jax.numpy as jnp
        import numpy as np
        B, T, DM = (2, 256, 128)
        DH = 128
        NH = DM // DH
        ROTARY_BASE = 10000.0

        def fractional_rope(x, base):
            dh = x.shape[-1]
            rot, skip = jnp.split(x, 2, axis=-1)
            width = rot.shape[-1]
            half = width // 2
            t = rot.shape[-2]
            positions = jnp.arange(t)[:, None]
            dims = jnp.arange(half)
            ang_freqs = jnp.power(base, -dims / half)[None, :]
            radians = positions * ang_freqs
            cos = jnp.cos(radians).astype(x.dtype)
            sin = jnp.sin(radians).astype(x.dtype)
            even, odd = jnp.split(rot, 2, axis=-1)
            r_even = even * cos - odd * sin
            r_odd = even * sin + odd * cos
            return jnp.concatenate([r_even, r_odd, skip], axis=-1)
        b, t, dm = x.shape
        q = jnp.einsum('btd,hdk->bhtk', x, wq)
        k = jnp.einsum('btd,hdk->bhtk', x, wk)
        v = jnp.einsum('btd,hdk->bhtk', x, wv)
        q = fractional_rope(q, ROTARY_BASE)
        k = fractional_rope(k, ROTARY_BASE)
        inv_sqrt_dh = DH ** (-0.5)
        q = q * inv_sqrt_dh
        k = k * inv_sqrt_dh
        s = jnp.einsum('bhik,bhjk->bhij', q, k)
        i = jnp.arange(t)[:, None]
        j = jnp.arange(t)[None, :]
        mask = jnp.less(i, j).astype(s.dtype)
        s = s - 1e+30 * mask
        p = jax.nn.softmax(s, axis=-1)
        o = jnp.einsum('bhij,bhjv->bihv', p, v)
        o = jnp.reshape(o, (b, t, NH * DH))
        return jnp.einsum('bto,od->btd', o, wo)

    def _L0_ffn_ref(x, w1, b1, w2, b2):
        import jax, jax.numpy as jnp
        import numpy as np

        def _binarize(w):
            alpha = jax.lax.stop_gradient(jnp.mean(jnp.abs(w), axis=1, keepdims=True))
            bw = alpha * jnp.sign(w)
            return w + jax.lax.stop_gradient(bw - w)
        bw1 = _binarize(w1)
        h = jnp.einsum('bsd,hd->bsh', x, bw1) + b1
        h = jax.nn.gelu(h, approximate=False)
        bw2 = _binarize(w2)
        out = jnp.einsum('bsh,dh->bsd', h, bw2) + b2
        return out
    x = L0_attn_x
    x = _layernorm(x + _L0_attn_ref(x, L0_attn_wq, L0_attn_wk, L0_attn_wv, L0_attn_wo), axis=-1)
    x = _layernorm(x + _L0_ffn_ref(x, L0_ffn_w1, L0_ffn_b1, L0_ffn_w2, L0_ffn_b2), axis=-1)
    return x

_drawn_inputs = setup_inputs


def setup_inputs(seed=0):
    import zlib

    import numpy as np

    out = dict(_drawn_inputs(seed))
    spreads = {}
    factors = {'L0_attn_wq': 6.157, 'L0_attn_wk': 6.087, 'L0_ffn_b1': 8.0, 'L0_ffn_b2': 2.786}
    for name, (base, spread) in spreads.items():
        noise = np.random.default_rng([zlib.crc32(name.encode()), seed]).standard_normal(out[name].shape)
        drawn = base * np.exp(spread * noise) if base else spread * noise
        out[name] = jnp.asarray(drawn.astype(out[name].dtype))
    for name, factor in factors.items():
        out[name] = (out[name] * factor).astype(out[name].dtype)
    return out
```

```python
import numpy as np
import concourse.bass as bass
from concourse import mybir
from contextlib import ExitStack

F32 = mybir.dt.float32
F32R = mybir.dt.float32r
BF16 = mybir.dt.bfloat16
ALU = mybir.AluOpType
ACT = mybir.ActivationFunctionType
AX = mybir.AxisListType

LN_EPS = 1e-5
MASKED = -1e30


def attention_ffn_kernel(nc, x, wq, wk, wv, wo, w1, b1, w2, b2, cos_t, sin_t, out):
    B, T, D = x.shape
    H = w1.shape[0]
    P = 128
    NT = T // P
    NF = H // P
    BANK = 512
    TG = BANK // P
    NG = NT // TG
    ROT = D // 2
    HALF = ROT // 2
    ROW = [P * (r * (r + 1) // 2) for r in range(NT + 1)]
    KEYS = [TG * (g + 1) for g in range(NG)]
    NPT = sum(KEYS)
    LN_STEPS = 9
    MEAN, RSTD = 2, 8

    ctx = ExitStack()
    with ctx:
        def sb(name, shape, dt=F32):
            return ctx.enter_context(nc.sbuf_tensor(name, shape, dt))

        def sem(name):
            return ctx.enter_context(nc.semaphore(name))

        ident = sb("ident", [P, P])
        ident_bf = sb("ident_bf", [P, P], BF16)
        mask_bf = sb("mask_bf", [P, P], BF16)
        minus_half = sb("minus_half", [P, NT])
        halves_c = sb("halves_c", [P, 2, NT])
        inv_d_c = sb("inv_d_c", [P, NT])
        eps_c = sb("eps_c", [P, NT])
        cos_sb = sb("cos_sb", [P, NT, 2, ROT])
        sin_sb = sb("sin_sb", [P, NT, 2, ROT])
        wqk = sb("wqk", [P, 2 * D])
        wqk_hi = sb("wqk_hi", [P, 2 * D], F32R)
        wqk_lo = sb("wqk_lo", [P, 2 * D], F32R)
        wv_sb = sb("wv_sb", [P, D])
        wvT = sb("wvT", [P, D])
        wo_sb = sb("wo_sb", [P, D])
        wvo = sb("wvo", [P, D])
        w1_sb = sb("w1_sb", [P, NF, D])
        w2_sb = sb("w2_sb", [P, H])
        neg1 = sb("neg1", [P, NF, D])
        neg2 = sb("neg2", [P, H])
        sgn1 = sb("sgn1", [P, NF, D])
        sgn2 = sb("sgn2", [P, H])
        sgn1T = sb("sgn1T", [P, NF, P], F32R)
        sgn2T = sb("sgn2T", [P, NF, D], F32R)
        sum1 = sb("sum1", [P, NF])
        sum2 = sb("sum2", [P, 1])
        alpha1 = sb("alpha1", [P, NF])
        alpha2 = sb("alpha2", [P, 1])
        b1_sb = sb("b1_sb", [P, NF])
        b2_sb = sb("b2_sb", [P, 1])
        xq = sb("xq", [P, NT, D])
        xT_hi = sb("xT_hi", [P, T], F32R)
        xT_lo = sb("xT_lo", [P, T], F32R)
        rot_cos = sb("rot_cos", [P, NT * 2, ROT])
        rot_sin = sb("rot_sin", [P, NT * 2, ROT])
        qk_tok = sb("qk_tok", [P, NT * 2, D])
        qkT_hi = sb("qkT_hi", [P, 2, T], F32R)
        qkT_lo = sb("qkT_lo", [P, 2, T], F32R)
        xa = sb("xa", [P, NT, D])
        negmax = sb("negmax", [P, NT])
        rowsum = sb("rowsum", [P, NT])
        rinv = sb("rinv", [P, NT])
        prob = sb("prob", [P, ROW[NT]])
        probT = [sb(f"probT{g}", [P, KEYS[g], BANK]) for g in range(NG)]
        pxT = sb("pxT", [P, NG, BANK])
        res1 = sb("res1", [P, NT, D])
        stat1 = sb("stat1", [P, NT, 6])
        ln1 = sb("ln1", [P, LN_STEPS, NT])
        x1 = sb("x1", [P, NT, D])
        x1T_hi = sb("x1T_hi", [P, T], F32R)
        x1T_lo = sb("x1T_lo", [P, T], F32R)
        hid = sb("hid", [P, NF, T])
        hid_hi = sb("hid_hi", [P, NF, T], F32R)
        hid_lo = sb("hid_lo", [P, NF, T], F32R)
        yT = sb("yT", [P, T])
        res2 = sb("res2", [P, NT, D])
        stat2 = sb("stat2", [P, NT, 6])
        ln2 = sb("ln2", [P, LN_STEPS, NT])
        y_out = sb("y_out", [P, NT, D])

        wide = [ctx.enter_context(nc.psum_tensor(f"wide{i}", [P, 2 * BANK], F32)) for i in range(2)]
        turn = [ctx.enter_context(nc.psum_tensor(f"turn{i}", [P, BANK], F32)) for i in range(2)]
        acc = [ctx.enter_context(nc.psum_tensor(f"acc{i}", [P, BANK], F32)) for i in range(2)]

        s_wqk_in, s_w_in = sem("s_wqk_in"), sem("s_w_in")
        s_xq_in, s_xa_in, s_stored = sem("s_xq_in"), sem("s_xa_in"), sem("s_stored")
        s_const, s_prep, s_prep_pe, s_prep_dve, s_weights = (
            sem("s_const"), sem("s_prep"), sem("s_prep_pe"), sem("s_prep_dve"), sem("s_weights"))
        s_xT, s_qk, s_qkT = sem("s_xT"), sem("s_qk"), sem("s_qkT")
        s_score, s_probT, s_px, s_proj = sem("s_score"), sem("s_probT"), sem("s_px"), sem("s_proj")
        s_x1T, s_up, s_down, s_yT = sem("s_x1T"), sem("s_up"), sem("s_down"), sem("s_yT")
        s_xT_hi, s_skip, s_qkT_hi = sem("s_xT_hi"), sem("s_skip"), sem("s_qkT_hi")
        s_exp, s_probT_out, s_px_out = sem("s_exp"), sem("s_probT_out"), sem("s_px_out")
        s_x1T_hi, s_gelu, s_y_out = sem("s_x1T_hi"), sem("s_gelu"), sem("s_y_out")
        s_xT_lo, s_rot_mul, s_qkT_lo = sem("s_xT_lo"), sem("s_rot_mul"), sem("s_qkT_lo")
        s_max, s_rinv, s_res1, s_stat1, s_x1 = sem("s_max"), sem("s_rinv"), sem("s_res1"), sem("s_stat1"), sem("s_x1")
        s_x1T_lo, s_hid_hi, s_res2, s_stat2, s_y = sem("s_x1T_lo"), sem("s_hid_hi"), sem("s_res2"), sem("s_stat2"), sem("s_y")
        s_rot_add, s_hid_lo, s_ln1, s_ln2 = sem("s_rot_add"), sem("s_hid_lo"), sem("s_ln1"), sem("s_ln2")

        def at(per, c, k):
            return per * c[0] + (per * c[1] + k)

        def run_steps(eng, step):
            for b in (-1, 0, 1):
                step(b)
            with eng.Fori(2, B - 1) as b:
                step(b)
            for b in (B - 1, B, B + 1):
                step(b)

        def stages(b):
            if not isinstance(b, int):
                return True, True, True, True
            return -1 <= b < B - 1, 0 <= b < B, 1 <= b <= B, 2 <= b <= B + 1

        block = ctx.enter_context(nc.Block())

        @block.sync
        def _(sp):
            sp.dma_start(xq[:, :, :], x[0].rearrange("(n p) d -> p n d", p=P)).then_inc(s_xq_in, 16)
            sp.dma_start(wqk[:, 0:D], wq[0]).then_inc(s_wqk_in, 16)
            sp.dma_start(wqk[:, D:2 * D], wk[0]).then_inc(s_wqk_in, 16)
            for j in range(2):
                sp.dma_start(cos_sb[:, :, j, :], cos_t.rearrange("(n p) d -> p n d", p=P)).then_inc(s_w_in, 16)
                sp.dma_start(sin_sb[:, :, j, :], sin_t.rearrange("(n p) d -> p n d", p=P)).then_inc(s_w_in, 16)
            sp.dma_start(wv_sb[:, :], wv[0]).then_inc(s_w_in, 16)
            sp.dma_start(wo_sb[:, :], wo).then_inc(s_w_in, 16)
            sp.dma_start(w1_sb[:, :, :], w1.rearrange("(p f) d -> p f d", f=NF)).then_inc(s_w_in, 16)
            sp.dma_start(w2_sb[:, :], w2).then_inc(s_w_in, 16)
            sp.dma_start(b1_sb[:, :], b1.rearrange("(p f) -> p f", f=NF)).then_inc(s_w_in, 16)
            sp.dma_start(b2_sb[:, :], b2.rearrange("(p a) -> p a", a=1)).then_inc(s_w_in, 16)

            def step(b):
                has_q, has_a, _, has_o = stages(b)
                if has_a:
                    if not (isinstance(b, int) and b == 0):
                        sp.wait_ge(s_res1, at(NT, (b, 0), 0))
                    sp.dma_start(xa[:, :, :], x[b].rearrange("(n p) d -> p n d", p=P)).then_inc(s_xa_in, 16)
                if has_q and has_a:
                    sp.wait_ge(s_xT, at(NG, (b, 0), NG))
                    sp.dma_start(xq[:, :, :], x[b + 1].rearrange("(n p) d -> p n d", p=P)).then_inc(s_xq_in, 16)
                if has_o:
                    sp.wait_ge(s_y, at(1, (b, -2), 1))
                    sp.dma_start(out[b - 2].rearrange("(n p) d -> p n d", p=P), y_out[:, :, :]).then_inc(s_stored, 16)

            run_steps(sp, step)
            sp.wait_ge(s_stored, 16 * B)

        @block.gpsimd
        def _(pool):
            pool.memset(ident[:, :], 0.0).then_inc(s_const, 1)
            pool.memset(ident_bf[:, :], 0.0).then_inc(s_const, 1)
            pool.memset(mask_bf[:, :], 0.0).then_inc(s_const, 1)
            for c, value in ((minus_half[:, :], -0.5), (halves_c[:, :, :], 0.5), (inv_d_c[:, :], 1.0 / D),
                             (eps_c[:, :], LN_EPS)):
                pool.memset(c, value).then_inc(s_const, 1)
            pool.wait_ge(s_const, 7)
            for m in (ident, ident_bf):
                pool.affine_select(out=m[:, :], in_=m[:, :], compare_op=ALU.not_equal, fill=1.0,
                                   base=0, pattern=[[-1, P]], channel_multiplier=1).then_inc(s_const, 1)
            pool.affine_select(out=mask_bf[:, :], in_=mask_bf[:, :], compare_op=ALU.is_ge, fill=MASKED,
                               base=0, pattern=[[-1, P]], channel_multiplier=1).then_inc(s_const, 1)

            def norm_factors(stat, ln, done, c):
                def after(n):
                    pool.wait_ge(done, at(LN_STEPS, c, n))

                mean_e, m2_e, mean_o, m2_o = (stat[:, :, j] for j in (1, 2, 4, 5))
                total, diff, mean, half, m2, part, half2, var, rstd = (ln[:, j, :] for j in range(LN_STEPS))
                pool.tensor_tensor(total, mean_e, mean_o, ALU.add).then_inc(done, 1)
                pool.tensor_tensor(diff, mean_e, mean_o, ALU.subtract).then_inc(done, 1)
                pool.tensor_tensor(m2, m2_e, m2_o, ALU.add).then_inc(done, 1)
                after(2)
                pool.tensor_tensor(ln[:, 2:4, :], ln[:, 0:2, :], halves_c[:, :, :], ALU.mult).then_inc(done, 1)
                after(3)
                pool.tensor_tensor(part, m2, inv_d_c[:, :], ALU.mult).then_inc(done, 1)
                after(4)
                pool.tensor_tensor(half2, half, half, ALU.mult).then_inc(done, 1)
                after(6)
                pool.tensor_tensor(var, part, half2, ALU.add).then_inc(done, 1)
                after(7)
                pool.tensor_tensor(var, var, eps_c[:, :], ALU.add).then_inc(done, 1)
                after(8)
                pool.tensor_tensor(rstd, var, minus_half[:, :], ALU.pow).then_inc(done, 1)

            def step(b):
                has_q, has_a, has_f, has_o = stages(b)
                q, a, f, o = (b, 1), (b, 0), (b, -1), (b, -2)
                if has_o:
                    pool.wait_ge(s_stat2, at(1, o, 1))
                    norm_factors(stat2, ln2, s_ln2, o)
                if has_f:
                    for j in range(NF):
                        pool.wait_ge(s_hid_hi, at(NF, f, j + 1))
                        pool.tensor_tensor(hid_lo[:, j, :], hid[:, j, :], hid_hi[:, j, :].bitcast(F32),
                                           ALU.subtract).then_inc(s_hid_lo, 1)
                if has_q:
                    for h in range(NG):
                        rows = slice(2 * TG * h, 2 * TG * (h + 1))
                        pool.wait_ge(s_rot_mul, at(NG, q, h + 1))
                        pool.tensor_tensor(qk_tok[:, rows, 0:ROT], rot_cos[:, rows, :], rot_sin[:, rows, :],
                                           ALU.add).then_inc(s_rot_add, 1)
                if has_a:
                    pool.wait_ge(s_stat1, at(1, a, 1))
                    norm_factors(stat1, ln1, s_ln1, a)

            run_steps(pool, step)

        def slot_of_probT(g, j):
            return sum(KEYS[:g]) + j

        @block.tensor
        def _(pe):
            pe.wait_ge(s_const, 10)
            pe.wait_ge(s_w_in, 16 * 10)
            pe.transpose(acc[0][:, 0:P], wv_sb[:, :], ident[:, :]).then_inc(s_prep_pe, 1)
            pe.wait_ge(s_prep, 1)
            for f in range(NF):
                ins = pe.transpose(turn[0][:, f * P:(f + 1) * P], sgn1[:, f, :], ident[:, :])
            ins.then_inc(s_prep_pe, 1)
            pe.wait_ge(s_prep, 2)
            for f in range(NF):
                ins = pe.transpose(turn[1][:, f * P:(f + 1) * P], sgn2[:, :].rearrange("d (p f) -> d f p", f=NF)[:, f, :], ident[:, :])
            ins.then_inc(s_prep_pe, 1)
            pe.wait_ge(s_prep, 3)
            pe.matmul(acc[1][:, 0:D], wvT[:, :], wo_sb[:, :], start=True, stop=True).then_inc(s_prep_pe, 1)
            pe.wait_ge(s_weights, 1)

            def step(b):
                has_q, has_a, has_f, _ = stages(b)
                q, a, f, o = (b, 1), (b, 0), (b, -1), (b, -2)
                first = isinstance(b, int) and b <= 1

                def scores(r):
                    n = 1 if r < TG else 2
                    if r in (0, TG):
                        pe.wait_ge(s_qkT_hi, at(2 * NG, a, 2 * n))
                        pe.wait_ge(s_qkT_lo, at(2 * NG, a, 2 * n))
                    if r >= 2:
                        pe.wait_ge(s_exp, at(NT, a, r - 1))
                    me = slice(r * P, (r + 1) * P)
                    parts = [(qkT_hi, qkT_hi), (qkT_hi, qkT_lo), (qkT_lo, qkT_hi)]
                    for lo in range(0, (r + 1) * P, BANK):
                        hi = min(lo + BANK, (r + 1) * P)
                        diagonal = hi == (r + 1) * P
                        for n, (qp, kp) in enumerate(parts):
                            ins = pe.matmul(wide[r % 2][:, lo:hi], qp[:, 0, me], kp[:, 1, lo:hi],
                                            start=n == 0, stop=n == 2 and not diagonal)
                        if diagonal:
                            ins = pe.matmul(wide[r % 2][:, hi - P:hi], ident_bf[:, :], mask_bf[:, :],
                                            start=False, stop=True)
                    ins.then_inc(s_score, 1)

                def turn_x1(h):
                    pe.wait_ge(s_x1, at(NG, f, h + 1))
                    if not first:
                        pe.wait_ge(s_res2, at(NG, o, h + 1))
                    for t in range(TG):
                        ins = pe.transpose(turn[h][:, t * P:(t + 1) * P], x1[:, TG * h + t, :], ident[:, :])
                    ins.then_inc(s_x1T, 1)

                def turn_prob(g, j):
                    u = slot_of_probT(g, j)
                    pe.wait_ge(s_exp, at(NT, a, TG * (g + 1)))
                    if u in (0, 1):
                        if has_f:
                            pe.wait_ge(s_x1T_lo, at(NG, f, u + 1))
                    elif g == 1 and j < 2 and has_q:
                        pe.wait_ge(s_xT_lo, at(NG, q, j + 1))
                    else:
                        pe.wait_ge(s_probT_out, at(NPT, a, u - 1))
                    for i in range(max(j, TG * g), TG * (g + 1)):
                        c = i - TG * g
                        ins = pe.transpose(turn[j % 2][:, c * P:(c + 1) * P],
                                           prob[:, ROW[i] + j * P:ROW[i] + (j + 1) * P], ident[:, :])
                    ins.then_inc(s_probT, 1)

                def weigh(g, j):
                    if g == 0 and j == 0:
                        pe.wait_ge(s_xa_in, at(16, a, 16))
                    pe.wait_ge(s_probT_out, at(NPT, a, slot_of_probT(g, j) + 1))
                    lo = max(j - TG * g, 0) * P
                    ins = pe.matmul(acc[g][:, lo:BANK], xa[:, j, :], probT[g][:, j, lo:BANK],
                                    start=j == 0, stop=j == KEYS[g] - 1)
                    if j == KEYS[g] - 1:
                        ins.then_inc(s_px, 1)

                def project_out(g):
                    pe.wait_ge(s_px_out, at(NG, a, g + 1))
                    for t in range(TG):
                        ins = pe.matmul(acc[g][:, t * D:(t + 1) * D], pxT[:, g, t * P:(t + 1) * P], wvo[:, :],
                                        start=True, stop=True)
                    ins.then_inc(s_proj, 1)

                def turn_x(h):
                    pe.wait_ge(s_xq_in, at(16, q, 16))
                    if has_a:
                        pe.wait_ge(s_probT_out, at(NPT, a, KEYS[0] - 1 + h))
                    for t in range(TG):
                        ins = pe.transpose(turn[h][:, t * P:(t + 1) * P], xq[:, TG * h + t, :], ident[:, :])
                    ins.then_inc(s_xT, 1)

                def up(j):
                    if j == 0:
                        pe.wait_ge(s_x1T_hi, at(NG, f, NG))
                        pe.wait_ge(s_x1T_lo, at(NG, f, NG))
                    if j >= 2:
                        pe.wait_ge(s_gelu, at(NF, f, j - 1))
                    elif has_a:
                        pe.wait_ge(s_exp, at(NT, a, NT - 1 + j))
                    for h in range(NG):
                        cols = slice(h * BANK, (h + 1) * BANK)
                        pe.matmul(wide[j % 2][:, cols], sgn1T[:, j, :], x1T_hi[:, cols], start=True, stop=False)
                        ins = pe.matmul(wide[j % 2][:, cols], sgn1T[:, j, :], x1T_lo[:, cols], start=False, stop=True)
                    ins.then_inc(s_up, 1)

                def project_qk(h):
                    pe.wait_ge(s_xT_hi, at(NG, q, h + 1))
                    pe.wait_ge(s_xT_lo, at(NG, q, h + 1))
                    if has_f:
                        pe.wait_ge(s_gelu, at(NF, f, 3 + h))
                    for t in range(TG):
                        me = slice((TG * h + t) * P, (TG * h + t + 1) * P)
                        cols = slice(t * 2 * D, (t + 1) * 2 * D)
                        pe.matmul(wide[h][:, cols], xT_hi[:, me], wqk_hi[:, :], start=True, stop=False)
                        pe.matmul(wide[h][:, cols], xT_hi[:, me], wqk_lo[:, :], start=False, stop=False)
                        ins = pe.matmul(wide[h][:, cols], xT_lo[:, me], wqk_hi[:, :], start=False, stop=True)
                    ins.then_inc(s_qk, 1)

                def down(j):
                    pe.wait_ge(s_hid_hi, at(NF, f, j + 1))
                    pe.wait_ge(s_hid_lo, at(NF, f, j + 1))
                    for h in range(NG):
                        if j == 0 and has_a:
                            pe.wait_ge(s_res1, at(NT, a, TG * (h + 1)))
                        cols = slice(h * BANK, (h + 1) * BANK)
                        pe.matmul(acc[h][:, :], sgn2T[:, j, :], hid_hi[:, j, cols], start=j == 0, stop=False)
                        ins = pe.matmul(acc[h][:, :], sgn2T[:, j, :], hid_lo[:, j, cols], start=False, stop=j == NF - 1)
                        if j == NF - 1:
                            ins.then_inc(s_down, 1)

                def turn_qk(n):
                    h = n // 2
                    pe.wait_ge(s_rot_add, at(NG, q, h + 1))
                    pe.wait_ge(s_skip, at(NG, q, h + 1))
                    if n >= 2:
                        pe.wait_ge(s_qkT_lo, at(2 * NG, q, n - 1))
                    elif has_a:
                        pe.wait_ge(s_probT_out, at(NPT, a, NPT - 1 + n))
                    for t in range(TG):
                        ins = pe.transpose(turn[n % 2][:, t * P:(t + 1) * P],
                                           qk_tok[:, 2 * (TG * h + t) + n % 2, :], ident[:, :])
                    ins.then_inc(s_qkT, 1)

                def turn_y(h):
                    pe.wait_ge(s_y_out, at(NG, f, h + 1))
                    if has_q:
                        pe.wait_ge(s_qkT_lo, at(2 * NG, q, 3 + h))
                    elif has_a:
                        pe.wait_ge(s_probT_out, at(NPT, a, NPT - 1 + h))
                    for t in range(TG):
                        me = slice((TG * h + t) * P, (TG * h + t + 1) * P)
                        ins = pe.transpose(turn[h][:, t * P:(t + 1) * P], yT[:, me], ident[:, :])
                    ins.then_inc(s_yT, 1)

                if has_a:
                    for r in range(6):
                        scores(r)
                if has_f:
                    turn_x1(0)
                    turn_x1(1)
                if has_a:
                    turn_prob(0, 0)
                    turn_prob(0, 1)
                    scores(6)
                    turn_prob(0, 2)
                    turn_prob(0, 3)
                    scores(7)
                    for j in range(KEYS[0]):
                        weigh(0, j)
                if has_q:
                    turn_x(0)
                    turn_x(1)
                if has_f:
                    up(0)
                if has_a:
                    for j in range(4):
                        turn_prob(1, j)
                if has_f:
                    up(1)
                if has_a:
                    for j in range(4, 8):
                        turn_prob(1, j)
                    for j in range(4):
                        weigh(1, j)
                if has_f:
                    up(2)
                if has_a:
                    for j in range(4, 8):
                        weigh(1, j)
                if has_f:
                    up(3)
                if has_a:
                    project_out(0)
                if has_q:
                    project_qk(0)
                if has_a:
                    project_out(1)
                if has_q:
                    project_qk(1)
                if has_f:
                    for j in range(3):
                        down(j)
                if has_q:
                    turn_qk(0)
                    turn_qk(1)
                if has_f:
                    down(3)
                if has_q:
                    turn_qk(2)
                    turn_qk(3)
                if has_f:
                    turn_y(0)
                    turn_y(1)

            run_steps(pe, step)

        @block.scalar
        def _(act):
            def step(b):
                has_q, has_a, has_f, _ = stages(b)
                q, a, f = (b, 1), (b, 0), (b, -1)

                def exponentials(r):
                    if r == 0 and not (isinstance(b, int) and b == 0):
                        act.wait_ge(s_rinv, at(1, a, 0))
                    act.wait_ge(s_max, at(NT, a, r + 1))
                    act.activation(prob[:, ROW[r]:ROW[r + 1]], wide[r % 2][:, 0:(r + 1) * P], ACT.Exp,
                                   bias=negmax[:, r:r + 1], accum_out=rowsum[:, r:r + 1]).then_inc(s_exp, 1)

                def probT_out(g, j):
                    act.wait_ge(s_probT, at(NPT, a, slot_of_probT(g, j) + 1))
                    lo = max(j - TG * g, 0) * P
                    act.activation(probT[g][:, j, lo:BANK], turn[j % 2][:, lo:BANK], ACT.Copy).then_inc(s_probT_out, 1)

                def high_part(dst, src, ready, per, c, k, done):
                    act.wait_ge(ready, at(per, c, k))
                    act.activation(dst, src, ACT.Copy).then_inc(done, 1)

                def gelu(j):
                    act.wait_ge(s_up, at(NF, f, j + 1))
                    act.activation(hid[:, j, :], wide[j % 2][:, :], ACT.Gelu, bias=b1_sb[:, j:j + 1],
                                   scale=alpha1[:, j:j + 1]).then_inc(s_gelu, 1)

                def px_out(g):
                    act.wait_ge(s_px, at(NG, a, g + 1))
                    act.activation(pxT[:, g, :], acc[g][:, :], ACT.Copy).then_inc(s_px_out, 1)

                def halves(h):
                    return slice(h * BANK, (h + 1) * BANK)

                if has_a:
                    for r in range(6):
                        exponentials(r)
                if has_f:
                    for h in range(NG):
                        high_part(x1T_hi[:, halves(h)], turn[h][:, :], s_x1T, NG, f, h + 1, s_x1T_hi)
                if has_a:
                    probT_out(0, 0)
                    probT_out(0, 1)
                    exponentials(6)
                    probT_out(0, 2)
                    probT_out(0, 3)
                    exponentials(7)
                    px_out(0)
                if has_q:
                    for h in range(NG):
                        high_part(xT_hi[:, halves(h)], turn[h][:, :], s_xT, NG, q, h + 1, s_xT_hi)
                if has_f:
                    if isinstance(b, int) and b == 1:
                        act.wait_ge(s_weights, 1)
                    gelu(0)
                if has_a:
                    for j in range(4):
                        probT_out(1, j)
                if has_f:
                    gelu(1)
                if has_a:
                    for j in range(4, 8):
                        probT_out(1, j)
                if has_f:
                    gelu(2)
                if has_a:
                    px_out(1)
                if has_f:
                    gelu(3)
                if has_q:
                    for h in range(NG):
                        act.wait_ge(s_rot_mul, at(NG, q, h + 1))
                        act.activation(qk_tok[:, 2 * TG * h:2 * TG * (h + 1), ROT:D],
                                       wide[h][:, :].rearrange("p (n d) -> p n d", d=D)[:, :, ROT:D],
                                       ACT.Copy).then_inc(s_skip, 1)
                    for n in range(2):
                        high_part(qkT_hi[:, n % 2, halves(n // 2)], turn[n % 2][:, :], s_qkT, 2 * NG, q, n + 1, s_qkT_hi)
                if has_f:
                    for h in range(NG):
                        act.wait_ge(s_down, at(NG, f, h + 1))
                        act.activation(yT[:, halves(h)], acc[h][:, :], ACT.Identity, bias=b2_sb[:, 0:1],
                                       scale=alpha2[:, 0:1]).then_inc(s_y_out, 1)
                if has_q:
                    for n in range(2, 4):
                        high_part(qkT_hi[:, n % 2, halves(n // 2)], turn[n % 2][:, :], s_qkT, 2 * NG, q, n + 1, s_qkT_hi)

            run_steps(act, step)

        @block.vector
        def _(dve):
            dve.wait_ge(s_wqk_in, 32)
            dve.tensor_scalar(wqk[:, 0:D], wqk[:, 0:D], 1.0 / D, None, ALU.mult).then_inc(s_prep_dve, 1)
            dve.wait_ge(s_prep_dve, 1)
            dve.tensor_copy(wqk_hi[:, :], wqk[:, :]).then_inc(s_prep_dve, 1)
            dve.wait_ge(s_prep_dve, 2)
            dve.tensor_tensor(wqk_lo[:, :], wqk[:, :], wqk_hi[:, :].bitcast(F32), ALU.subtract).then_inc(s_prep_dve, 1)
            dve.wait_ge(s_w_in, 16 * 10)
            dve.tensor_scalar(neg1[:, :, :], w1_sb[:, :, :], 0.0, None, ALU.is_lt).then_inc(s_prep_dve, 1)
            dve.tensor_scalar(neg2[:, :], w2_sb[:, :], 0.0, None, ALU.is_lt).then_inc(s_prep_dve, 1)
            dve.wait_ge(s_prep_dve, 5)
            dve.scalar_tensor_tensor(sgn1[:, :, :], w1_sb[:, :, :], 0.0, neg1[:, :, :], ALU.is_gt, ALU.subtract).then_inc(s_prep, 1)
            dve.scalar_tensor_tensor(sgn2[:, :], w2_sb[:, :], 0.0, neg2[:, :], ALU.is_gt, ALU.subtract).then_inc(s_prep, 1)
            dve.wait_ge(s_prep_pe, 1)
            dve.tensor_copy(wvT[:, :], acc[0][:, 0:P]).then_inc(s_prep, 1)
            dve.tensor_reduce(sum1[:, :], w1_sb[:, :, :], axis=AX.X, op=ALU.add, apply_absolute_value=True).then_inc(s_prep_dve, 1)
            dve.tensor_reduce(sum2[:, :], w2_sb[:, :], axis=AX.X, op=ALU.add, apply_absolute_value=True).then_inc(s_prep_dve, 1)
            dve.wait_ge(s_prep_dve, 7)
            dve.tensor_scalar(alpha1[:, :], sum1[:, :], 1.0 / D, None, ALU.mult)
            dve.tensor_scalar(alpha2[:, :], sum2[:, :], 1.0 / H, None, ALU.mult)
            dve.wait_ge(s_prep_pe, 2)
            dve.tensor_copy(sgn1T[:, :, :].rearrange("p f m -> p (f m)"), turn[0][:, :])
            dve.wait_ge(s_prep_pe, 3)
            dve.tensor_copy(sgn2T[:, :, :].rearrange("p f m -> p (f m)"), turn[1][:, :])
            dve.wait_ge(s_prep_pe, 4)
            dve.tensor_copy(wvo[:, :], acc[1][:, 0:D]).then_inc(s_weights, 1)

            def step(b):
                has_q, has_a, has_f, has_o = stages(b)
                q, a, f, o = (b, 1), (b, 0), (b, -1), (b, -2)

                def halves(h):
                    return slice(h * BANK, (h + 1) * BANK)

                def row_max(r):
                    dve.wait_ge(s_score, at(NT, a, r + 1))
                    dve.tensor_reduce(negmax[:, r:r + 1], wide[r % 2][:, 0:(r + 1) * P], axis=AX.X, op=ALU.max,
                                      negate=True).then_inc(s_max, 1)

                def low_part(dst, src, high, ready, per, c, k, done):
                    dve.wait_ge(ready, at(per, c, k))
                    dve.tensor_tensor(dst, src, high.bitcast(F32), ALU.subtract).then_inc(done, 1)

                def hidden_high(j):
                    dve.wait_ge(s_gelu, at(NF, f, j + 1))
                    dve.tensor_copy(hid_hi[:, j, :], hid[:, j, :]).then_inc(s_hid_hi, 1)

                def rotate(h):
                    rows = slice(2 * TG * h, 2 * TG * (h + 1))
                    pairs = wide[h][:, :].rearrange("p (n d) -> p n d", d=D)
                    cos_h = cos_sb[:, :, :, :].rearrange("p n j d -> p (n j) d")[:, rows, :]
                    sin_h = sin_sb[:, :, :, :].rearrange("p n j d -> p (n j) d")[:, rows, :]
                    dve.wait_ge(s_qk, at(NG, q, h + 1))
                    dve.tensor_tensor(rot_cos[:, rows, :], pairs[:, :, 0:ROT], cos_h, ALU.mult)
                    dve.tensor_tensor(rot_sin[:, rows, 0:HALF], pairs[:, :, HALF:ROT], sin_h[:, :, 0:HALF], ALU.mult)
                    dve.tensor_tensor(rot_sin[:, rows, HALF:ROT], pairs[:, :, 0:HALF], sin_h[:, :, HALF:ROT],
                                      ALU.mult).then_inc(s_rot_mul, 1)

                def residual1(g):
                    dve.wait_ge(s_proj, at(NG, a, g + 1))
                    if g == 0 and has_f:
                        dve.wait_ge(s_x1, at(NG, f, NG))
                    for t in range(TG * g, TG * (g + 1)):
                        c = t - TG * g
                        dve.scalar_tensor_tensor(res1[:, t, :], acc[g][:, c * D:(c + 1) * D], rinv[:, t:t + 1],
                                                 xa[:, t, :], ALU.mult, ALU.add).then_inc(s_res1, 1)

                def residual2(h):
                    dve.wait_ge(s_yT, at(NG, f, h + 1))
                    if h == 0 and has_o:
                        dve.wait_ge(s_y, at(1, o, 1))
                    dve.tensor_tensor(res2[:, TG * h:TG * (h + 1), :],
                                      turn[h][:, :].rearrange("p (n d) -> p n d", d=D),
                                      x1[:, TG * h:TG * (h + 1), :], ALU.add).then_inc(s_res2, 1)

                def statistics(res, stat, ready, per, c, done):
                    dve.wait_ge(ready, at(per, c, per))
                    for t in range(NT):
                        ins = dve.bn_stats(stat[:, t, :], res[:, t, :])
                    ins.then_inc(done, 1)

                def normalize(dst, res, ln, t):
                    return dve.tensor_scalar(dst[:, t, :], res[:, t, :], ln[:, MEAN, t:t + 1],
                                             ln[:, RSTD, t:t + 1], ALU.subtract, ALU.mult)

                if has_a:
                    for r in range(6):
                        row_max(r)
                if has_f:
                    for h in range(NG):
                        low_part(x1T_lo[:, halves(h)], turn[h][:, :], x1T_hi[:, halves(h)], s_x1T_hi, NG, f, h + 1, s_x1T_lo)
                if has_a:
                    row_max(6)
                    row_max(7)
                if has_o:
                    dve.wait_ge(s_ln2, at(LN_STEPS, o, LN_STEPS))
                    if not (isinstance(b, int) and b == 2):
                        dve.wait_ge(s_stored, at(16, o, 0))
                    for t in range(NT):
                        ins = normalize(y_out, res2, ln2, t)
                    ins.then_inc(s_y, 1)
                if has_q:
                    for h in range(NG):
                        low_part(xT_lo[:, halves(h)], turn[h][:, :], xT_hi[:, halves(h)], s_xT_hi, NG, q, h + 1, s_xT_lo)
                if has_a:
                    dve.wait_ge(s_exp, at(NT, a, NT))
                    dve.reciprocal(rinv[:, :], rowsum[:, :]).then_inc(s_rinv, 1)
                if has_f:
                    for j in range(3):
                        hidden_high(j)
                if has_a:
                    dve.wait_ge(s_rinv, at(1, a, 1))
                    residual1(0)
                if has_f:
                    hidden_high(3)
                if has_q:
                    rotate(0)
                if has_a:
                    residual1(1)
                if has_q:
                    rotate(1)
                if has_a:
                    statistics(res1, stat1, s_res1, NT, a, s_stat1)
                if has_q:
                    for n in range(4):
                        h, j = n // 2, n % 2
                        low_part(qkT_lo[:, j, halves(h)], turn[j][:, :], qkT_hi[:, j, halves(h)],
                                 s_qkT_hi, 2 * NG, q, n + 1, s_qkT_lo)
                if has_f:
                    residual2(0)
                    residual2(1)
                if has_a:
                    dve.wait_ge(s_ln1, at(LN_STEPS, a, LN_STEPS))
                    if has_f:
                        dve.wait_ge(s_res2, at(NG, f, NG))
                    for h in range(NG):
                        for t in range(TG * h, TG * (h + 1)):
                            ins = normalize(x1, res1, ln1, t)
                        ins.then_inc(s_x1, 1)
                if has_f:
                    statistics(res2, stat2, s_res2, NG, f, s_stat2)

            run_steps(dve, step)


def rotation_tables(T, D, base=10000.0):
    half = D // 4
    freqs = np.power(np.float32(base), -np.arange(half, dtype=np.float32) / np.float32(half), dtype=np.float32)
    radians = np.arange(T, dtype=np.float32)[:, None] * freqs[None, :]
    cos, sin = np.cos(radians), np.sin(radians)
    return (np.concatenate([cos, cos], axis=1).astype(np.float32),
            np.concatenate([-sin, sin], axis=1).astype(np.float32))


_INS = ['L0_attn_x', 'L0_attn_wq', 'L0_attn_wk', 'L0_attn_wv', 'L0_attn_wo',
        'L0_ffn_w1', 'L0_ffn_b1', 'L0_ffn_w2', 'L0_ffn_b2']


def kernel(**inputs):
    import concourse.bacc as _bacc
    from concourse.bass_utils import run_bass_kernel_spmd as _run

    nc = _bacc.Bacc("TRN2", target_bir_lowering=False, num_devices=1)
    given = {name: np.ascontiguousarray(inputs[name]) for name in _INS}
    given["cos"], given["sin"] = rotation_tables(given['L0_attn_x'].shape[1], given['L0_attn_x'].shape[2])
    arrays, args = {}, []
    for name, a in given.items():
        arrays[f"in_{name}_dram"] = a
        args.append(nc.dram_tensor(f"in_{name}_dram", a.shape, mybir.dt.from_np(a.dtype), kind="ExternalInput").ap())
    shape = given['L0_attn_x'].shape
    args.append(nc.dram_tensor("out_0_dram", shape, F32, kind="ExternalOutput").ap())
    attention_ffn_kernel(nc, *args)
    r = _run(nc, [arrays], core_ids=[0])
    return r.results[0]["out_0_dram"]
```

```python
import numpy as np
import concourse.bass as bass
from concourse import mybir
from contextlib import ExitStack

F32 = mybir.dt.float32
F32R = mybir.dt.float32r
BF16 = mybir.dt.bfloat16
ALU = mybir.AluOpType
ACT = mybir.ActivationFunctionType
AX = mybir.AxisListType

LN_EPS = 1e-5
MASKED = -1e30


def attention_ffn_kernel(nc, x, wq, wk, wv, wo, w1, b1, w2, b2, cos_t, sin_t, out):
    B, T, D = x.shape
    H = w1.shape[0]
    P = 128
    NT = T // P
    NF = H // P
    BANK = 512
    TG = BANK // P
    NG = NT // TG
    ROT = D // 2
    HALF = ROT // 2
    ROW = [P * (r * (r + 1) // 2) for r in range(NT + 1)]
    KEYS = [TG * (g + 1) for g in range(NG)]
    NPT = sum(KEYS)
    ACT_PT = NPT - 4
    DVE_PT = NPT - ACT_PT
    LN_STEPS = 9
    MEAN, RSTD = 2, 8

    ctx = ExitStack()
    with ctx:
        def sb(name, shape, dt=F32):
            return ctx.enter_context(nc.sbuf_tensor(name, shape, dt))

        def sem(name):
            return ctx.enter_context(nc.semaphore(name))

        ident = sb("ident", [P, P])
        ident_bf = sb("ident_bf", [P, P], BF16)
        mask_bf = sb("mask_bf", [P, P], BF16)
        minus_half = sb("minus_half", [P, NT])
        halves_c = sb("halves_c", [P, 2, NT])
        inv_d_c = sb("inv_d_c", [P, NT])
        eps_c = sb("eps_c", [P, NT])
        cos_sb = sb("cos_sb", [P, NT, 2, ROT])
        sin_sb = sb("sin_sb", [P, NT, 2, ROT])
        wqk = sb("wqk", [P, 2 * D])
        wqk_hi = sb("wqk_hi", [P, 2 * D], F32R)
        wqk_lo = sb("wqk_lo", [P, 2 * D], F32R)
        wv_sb = sb("wv_sb", [P, D])
        wvT = sb("wvT", [P, D])
        wo_sb = sb("wo_sb", [P, D])
        wvo = sb("wvo", [P, D])
        w1_sb = sb("w1_sb", [P, NF, D])
        w2_sb = sb("w2_sb", [P, H])
        neg1 = sb("neg1", [P, NF, D])
        neg2 = sb("neg2", [P, H])
        sgn1 = sb("sgn1", [P, NF, D])
        sgn2 = sb("sgn2", [P, H])
        sgn1T = sb("sgn1T", [P, NF, P], F32R)
        sgn2T = sb("sgn2T", [P, NF, D], F32R)
        sum1 = sb("sum1", [P, NF])
        sum2 = sb("sum2", [P, 1])
        alpha1 = sb("alpha1", [P, NF])
        alpha2 = sb("alpha2", [P, 1])
        b1_sb = sb("b1_sb", [P, NF])
        b2_sb = sb("b2_sb", [P, 1])
        xq = sb("xq", [P, NT, D])
        xT_hi = sb("xT_hi", [P, T], F32R)
        xT_lo = sb("xT_lo", [P, T], F32R)
        rot_cos = sb("rot_cos", [P, NT * 2, ROT])
        rot_sin = sb("rot_sin", [P, NT * 2, ROT])
        qk_tok = sb("qk_tok", [P, NT * 2, D])
        qkT_hi = sb("qkT_hi", [P, 2, T], F32R)
        qkT_lo = sb("qkT_lo", [P, 2, T], F32R)
        xa = sb("xa", [P, NT, D])
        negmax = sb("negmax", [P, NT])
        rowsum = sb("rowsum", [P, NT])
        rinv = sb("rinv", [P, NT])
        prob = sb("prob", [P, ROW[NT]])
        probT = [sb(f"probT{g}", [P, KEYS[g], BANK]) for g in range(NG)]
        pxT = sb("pxT", [P, NG, BANK])
        res1 = sb("res1", [P, NT, D])
        stat1 = sb("stat1", [P, NT, 6])
        ln1 = sb("ln1", [P, LN_STEPS, NT])
        x1 = sb("x1", [P, NT, D])
        x1T_hi = sb("x1T_hi", [P, T], F32R)
        x1T_lo = sb("x1T_lo", [P, T], F32R)
        hid = sb("hid", [P, NF, T])
        hid_hi = sb("hid_hi", [P, NF, T], F32R)
        hid_lo = sb("hid_lo", [P, NF, T], F32R)
        yT = sb("yT", [P, T])
        res2 = sb("res2", [P, NT, D])
        stat2 = sb("stat2", [P, NT, 6])
        ln2 = sb("ln2", [P, LN_STEPS, NT])
        y_out = sb("y_out", [P, NT, D])

        wide = [ctx.enter_context(nc.psum_tensor(f"wide{i}", [P, 2 * BANK], F32)) for i in range(2)]
        turn = [ctx.enter_context(nc.psum_tensor(f"turn{i}", [P, BANK], F32)) for i in range(2)]
        acc = [ctx.enter_context(nc.psum_tensor(f"acc{i}", [P, BANK], F32)) for i in range(2)]

        s_wqk_in, s_w_in = sem("s_wqk_in"), sem("s_w_in")
        s_xq_in, s_xa_in, s_stored = sem("s_xq_in"), sem("s_xa_in"), sem("s_stored")
        s_const, s_prep, s_prep_pe, s_prep_dve, s_weights = (
            sem("s_const"), sem("s_prep"), sem("s_prep_pe"), sem("s_prep_dve"), sem("s_weights"))
        s_xT, s_qk, s_qkT = sem("s_xT"), sem("s_qk"), sem("s_qkT")
        s_score, s_probT, s_px, s_proj = sem("s_score"), sem("s_probT"), sem("s_px"), sem("s_proj")
        s_x1T, s_up, s_down, s_yT = sem("s_x1T"), sem("s_up"), sem("s_down"), sem("s_yT")
        s_xT_hi, s_skip, s_qkT_hi = sem("s_xT_hi"), sem("s_skip"), sem("s_qkT_hi")
        s_exp, s_probT_act, s_px_out = sem("s_exp"), sem("s_probT_act"), sem("s_px_out")
        s_x1T_hi, s_gelu, s_y_out = sem("s_x1T_hi"), sem("s_gelu"), sem("s_y_out")
        s_xT_lo, s_rot_mul, s_qkT_lo = sem("s_xT_lo"), sem("s_rot_mul"), sem("s_qkT_lo")
        s_max, s_rinv, s_res1, s_stat1, s_x1 = sem("s_max"), sem("s_rinv"), sem("s_res1"), sem("s_stat1"), sem("s_x1")
        s_probT_dve = sem("s_probT_dve")
        s_x1T_lo, s_hid_hi, s_res2, s_stat2, s_y = sem("s_x1T_lo"), sem("s_hid_hi"), sem("s_res2"), sem("s_stat2"), sem("s_y")
        s_rot_add, s_hid_lo, s_ln1, s_ln2 = sem("s_rot_add"), sem("s_hid_lo"), sem("s_ln1"), sem("s_ln2")

        def at(per, c, k):
            return per * c[0] + (per * c[1] + k)

        def run_steps(eng, step):
            for b in range(-1, 3):
                step(b)
            with eng.Fori(3, B - 1) as b:
                step(b)
            for b in range(B - 1, B + 3):
                step(b)

        def stages(b):
            if not isinstance(b, int):
                return True, True, True, True, True
            return -1 <= b < B - 1, 0 <= b < B, 1 <= b <= B, 2 <= b <= B + 1, 3 <= b <= B + 2

        block = ctx.enter_context(nc.Block())

        @block.sync
        def _(sp):
            sp.dma_start(xq[:, :, :], x[0].rearrange("(n p) d -> p n d", p=P)).then_inc(s_xq_in, 16)
            sp.dma_start(wqk[:, 0:D], wq[0]).then_inc(s_wqk_in, 16)
            sp.dma_start(wqk[:, D:2 * D], wk[0]).then_inc(s_wqk_in, 16)
            for j in range(2):
                sp.dma_start(cos_sb[:, :, j, :], cos_t.rearrange("(n p) d -> p n d", p=P)).then_inc(s_w_in, 16)
                sp.dma_start(sin_sb[:, :, j, :], sin_t.rearrange("(n p) d -> p n d", p=P)).then_inc(s_w_in, 16)
            sp.dma_start(wv_sb[:, :], wv[0]).then_inc(s_w_in, 16)
            sp.dma_start(wo_sb[:, :], wo).then_inc(s_w_in, 16)
            sp.dma_start(w1_sb[:, :, :], w1.rearrange("(p f) d -> p f d", f=NF)).then_inc(s_w_in, 16)
            sp.dma_start(w2_sb[:, :], w2).then_inc(s_w_in, 16)
            sp.dma_start(b1_sb[:, :], b1.rearrange("(p f) -> p f", f=NF)).then_inc(s_w_in, 16)
            sp.dma_start(b2_sb[:, :], b2.rearrange("(p a) -> p a", a=1)).then_inc(s_w_in, 16)

            def step(b):
                has_q, has_a, _, _, has_z = stages(b)
                if has_q and has_a:
                    sp.wait_ge(s_xT, at(NG, (b, 0), NG))
                    sp.dma_start(xq[:, :, :], x[b + 1].rearrange("(n p) d -> p n d", p=P)).then_inc(s_xq_in, 16)
                if has_a:
                    if not (isinstance(b, int) and b == 0):
                        sp.wait_ge(s_res1, at(NT, (b, 0), 0))
                    sp.dma_start(xa[:, :, :], x[b].rearrange("(n p) d -> p n d", p=P)).then_inc(s_xa_in, 16)
                if has_z:
                    sp.wait_ge(s_y, at(1, (b, -3), 1))
                    sp.dma_start(out[b - 3].rearrange("(n p) d -> p n d", p=P), y_out[:, :, :]).then_inc(s_stored, 16)

            run_steps(sp, step)
            sp.wait_ge(s_stored, 16 * B)

        @block.gpsimd
        def _(pool):
            pool.memset(ident[:, :], 0.0).then_inc(s_const, 1)
            pool.memset(ident_bf[:, :], 0.0).then_inc(s_const, 1)
            pool.memset(mask_bf[:, :], 0.0).then_inc(s_const, 1)
            for c, value in ((minus_half[:, :], -0.5), (halves_c[:, :, :], 0.5), (inv_d_c[:, :], 1.0 / D),
                             (eps_c[:, :], LN_EPS)):
                pool.memset(c, value).then_inc(s_const, 1)
            pool.wait_ge(s_const, 7)
            for m in (ident, ident_bf):
                pool.affine_select(out=m[:, :], in_=m[:, :], compare_op=ALU.not_equal, fill=1.0,
                                   base=0, pattern=[[-1, P]], channel_multiplier=1).then_inc(s_const, 1)
            pool.affine_select(out=mask_bf[:, :], in_=mask_bf[:, :], compare_op=ALU.is_ge, fill=MASKED,
                               base=0, pattern=[[-1, P]], channel_multiplier=1).then_inc(s_const, 1)

            def norm_factors(stat, ln, done, c):
                def after(n):
                    pool.wait_ge(done, at(LN_STEPS, c, n))

                mean_e, m2_e, mean_o, m2_o = (stat[:, :, j] for j in (1, 2, 4, 5))
                total, diff, mean, half, m2, part, half2, var, rstd = (ln[:, j, :] for j in range(LN_STEPS))
                pool.tensor_tensor(total, mean_e, mean_o, ALU.add).then_inc(done, 1)
                pool.tensor_tensor(diff, mean_e, mean_o, ALU.subtract).then_inc(done, 1)
                pool.tensor_tensor(m2, m2_e, m2_o, ALU.add).then_inc(done, 1)
                after(2)
                pool.tensor_tensor(ln[:, 2:4, :], ln[:, 0:2, :], halves_c[:, :, :], ALU.mult).then_inc(done, 1)
                after(3)
                pool.tensor_tensor(part, m2, inv_d_c[:, :], ALU.mult).then_inc(done, 1)
                after(4)
                pool.tensor_tensor(half2, half, half, ALU.mult).then_inc(done, 1)
                after(6)
                pool.tensor_tensor(var, part, half2, ALU.add).then_inc(done, 1)
                after(7)
                pool.tensor_tensor(var, var, eps_c[:, :], ALU.add).then_inc(done, 1)
                after(8)
                pool.tensor_tensor(rstd, var, minus_half[:, :], ALU.pow).then_inc(done, 1)

            def step(b):
                has_q, has_a, has_f, has_o, has_z = stages(b)
                q, f, z = (b, 1), (b, -1), (b, -3)
                if has_z:
                    pool.wait_ge(s_stat2, at(1, z, 1))
                    norm_factors(stat2, ln2, s_ln2, z)
                if has_f:
                    pool.wait_ge(s_stat1, at(1, f, 1))
                    norm_factors(stat1, ln1, s_ln1, f)
                if has_q:
                    for h in range(NG):
                        rows = slice(2 * TG * h, 2 * TG * (h + 1))
                        pool.wait_ge(s_rot_mul, at(NG, q, h + 1))
                        pool.tensor_tensor(qk_tok[:, rows, 0:ROT], rot_cos[:, rows, :], rot_sin[:, rows, :],
                                           ALU.add).then_inc(s_rot_add, 1)
                if has_f:
                    for j in range(NF):
                        pool.wait_ge(s_hid_hi, at(NF, f, j + 1))
                        pool.tensor_tensor(hid_lo[:, j, :], hid[:, j, :], hid_hi[:, j, :].bitcast(F32),
                                           ALU.subtract).then_inc(s_hid_lo, 1)

            run_steps(pool, step)

        def slot_of_probT(g, j):
            return sum(KEYS[:g]) + j

        @block.tensor
        def _(pe):
            pe.wait_ge(s_const, 10)
            pe.wait_ge(s_w_in, 16 * 10)
            pe.transpose(acc[0][:, 0:P], wv_sb[:, :], ident[:, :]).then_inc(s_prep_pe, 1)
            pe.wait_ge(s_prep, 1)
            for f in range(NF):
                ins = pe.transpose(turn[0][:, f * P:(f + 1) * P], sgn1[:, f, :], ident[:, :])
            ins.then_inc(s_prep_pe, 1)
            pe.wait_ge(s_prep, 2)
            for f in range(NF):
                ins = pe.transpose(turn[1][:, f * P:(f + 1) * P], sgn2[:, :].rearrange("d (p f) -> d f p", f=NF)[:, f, :], ident[:, :])
            ins.then_inc(s_prep_pe, 1)
            pe.wait_ge(s_prep, 3)
            pe.matmul(acc[1][:, 0:D], wvT[:, :], wo_sb[:, :], start=True, stop=True).then_inc(s_prep_pe, 1)
            pe.wait_ge(s_weights, 1)

            def step(b):
                has_q, has_a, has_f, has_o, has_z = stages(b)
                q, a, f, o, z = (b, 1), (b, 0), (b, -1), (b, -2), (b, -3)

                def scores(r):
                    n = 1 if r < TG else 2
                    if r in (0, TG):
                        pe.wait_ge(s_qkT_hi, at(2 * NG, a, 2 * n))
                        pe.wait_ge(s_qkT_lo, at(2 * NG, a, 2 * n))
                    if r >= 2:
                        pe.wait_ge(s_exp, at(NT, a, r - 1))
                    elif has_o:
                        pe.wait_ge(s_gelu, at(NF, o, 3 + r))
                    me = slice(r * P, (r + 1) * P)
                    parts = [(qkT_hi, qkT_hi), (qkT_hi, qkT_lo), (qkT_lo, qkT_hi)]
                    for lo in range(0, (r + 1) * P, BANK):
                        hi = min(lo + BANK, (r + 1) * P)
                        diagonal = hi == (r + 1) * P
                        for n, (qp, kp) in enumerate(parts):
                            ins = pe.matmul(wide[r % 2][:, lo:hi], qp[:, 0, me], kp[:, 1, lo:hi],
                                            start=n == 0, stop=n == 2 and not diagonal)
                        if diagonal:
                            ins = pe.matmul(wide[r % 2][:, hi - P:hi], ident_bf[:, :], mask_bf[:, :],
                                            start=False, stop=True)
                    ins.then_inc(s_score, 1)

                def turn_x1(h):
                    pe.wait_ge(s_x1, at(NG, f, h + 1))
                    if has_a:
                        wait_probT_read(1, h)
                    else:
                        pe.wait_ge(s_res2, at(NG, o, h + 1))
                    for t in range(TG):
                        ins = pe.transpose(turn[h][:, t * P:(t + 1) * P], x1[:, TG * h + t, :], ident[:, :])
                    ins.then_inc(s_x1T, 1)

                def wait_probT_read(g, j):
                    u = slot_of_probT(g, j)
                    if u < ACT_PT:
                        pe.wait_ge(s_probT_act, at(ACT_PT, a, u + 1))
                    else:
                        pe.wait_ge(s_probT_dve, at(DVE_PT, a, u + 1 - ACT_PT))

                def turn_prob(g, j):
                    u = slot_of_probT(g, j)
                    pe.wait_ge(s_exp, at(NT, a, TG * (g + 1)))
                    if g == 1 and j in (0, 1) and has_o:
                        pe.wait_ge(s_res2, at(NG, o, j + 1))
                    elif g == 1 and j in (0, 1):
                        pe.wait_ge(s_xT_lo, at(NG, q, j + 1))
                    elif g == 1 and j in (2, 3) and has_f:
                        pe.wait_ge(s_x1T_lo, at(NG, f, j - 1))
                    elif u >= 2:
                        wait_probT_read(g if j >= 2 else g - 1, j - 2 if j >= 2 else KEYS[g - 1] - 2 + j)
                    for i in range(max(j, TG * g), TG * (g + 1)):
                        c = i - TG * g
                        ins = pe.transpose(turn[j % 2][:, c * P:(c + 1) * P],
                                           prob[:, ROW[i] + j * P:ROW[i] + (j + 1) * P], ident[:, :])
                    ins.then_inc(s_probT, 1)

                def weigh(g, j, c):
                    if g == 0 and j == 0:
                        pe.wait_ge(s_xa_in, at(16, c, 16))
                        if has_o:
                            pe.wait_ge(s_y_out, at(NG, o, 1))
                    u = slot_of_probT(g, j)
                    if u < ACT_PT:
                        pe.wait_ge(s_probT_act, at(ACT_PT, c, u + 1))
                    else:
                        pe.wait_ge(s_probT_dve, at(DVE_PT, c, u + 1 - ACT_PT))
                    lo = max(j - TG * g, 0) * P
                    ins = pe.matmul(acc[g][:, lo:BANK], xa[:, j, :], probT[g][:, j, lo:BANK],
                                    start=j == 0, stop=j == KEYS[g] - 1)
                    if j == KEYS[g] - 1:
                        ins.then_inc(s_px, 1)

                def project_out(g, c):
                    pe.wait_ge(s_px_out, at(NG, c, g + 1))
                    for t in range(TG):
                        ins = pe.matmul(acc[g][:, t * D:(t + 1) * D], pxT[:, g, t * P:(t + 1) * P], wvo[:, :],
                                        start=True, stop=True)
                    ins.then_inc(s_proj, 1)

                def turn_x(h):
                    pe.wait_ge(s_xq_in, at(16, q, 16))
                    if has_a:
                        wait_probT_read(0, KEYS[0] - 2 + h)
                    for t in range(TG):
                        ins = pe.transpose(turn[h][:, t * P:(t + 1) * P], xq[:, TG * h + t, :], ident[:, :])
                    ins.then_inc(s_xT, 1)

                def up(j):
                    if j == 0:
                        pe.wait_ge(s_x1T_hi, at(NG, f, NG))
                        pe.wait_ge(s_x1T_lo, at(NG, f, NG))
                    if j >= 2:
                        pe.wait_ge(s_gelu, at(NF, f, j - 1))
                    elif has_q:
                        pe.wait_ge(s_rot_mul, at(NG, q, j + 1))
                        pe.wait_ge(s_skip, at(NG, q, j + 1))
                    elif has_a:
                        pe.wait_ge(s_exp, at(NT, a, NT - 1 + j))
                    else:
                        pe.wait_ge(s_gelu, at(NF, o, 3 + j))
                    for h in range(NG):
                        cols = slice(h * BANK, (h + 1) * BANK)
                        pe.matmul(wide[j % 2][:, cols], sgn1T[:, j, :], x1T_hi[:, cols], start=True, stop=False)
                        ins = pe.matmul(wide[j % 2][:, cols], sgn1T[:, j, :], x1T_lo[:, cols], start=False, stop=True)
                    ins.then_inc(s_up, 1)

                def project_qk(h):
                    pe.wait_ge(s_xT_hi, at(NG, q, h + 1))
                    pe.wait_ge(s_xT_lo, at(NG, q, h + 1))
                    if has_a:
                        pe.wait_ge(s_exp, at(NT, a, NT - 1 + h))
                    for t in range(TG):
                        me = slice((TG * h + t) * P, (TG * h + t + 1) * P)
                        cols = slice(t * 2 * D, (t + 1) * 2 * D)
                        pe.matmul(wide[h][:, cols], xT_hi[:, me], wqk_hi[:, :], start=True, stop=False)
                        pe.matmul(wide[h][:, cols], xT_hi[:, me], wqk_lo[:, :], start=False, stop=False)
                        ins = pe.matmul(wide[h][:, cols], xT_lo[:, me], wqk_hi[:, :], start=False, stop=True)
                    ins.then_inc(s_qk, 1)

                def down(h):
                    if has_f:
                        pe.wait_ge(s_res1, at(NT, f, TG * (h + 1)))
                    cols = slice(h * BANK, (h + 1) * BANK)
                    for j in range(NF):
                        pe.wait_ge(s_hid_hi, at(NF, o, j + 1))
                        pe.wait_ge(s_hid_lo, at(NF, o, j + 1))
                        pe.matmul(acc[h][:, :], sgn2T[:, j, :], hid_hi[:, j, cols], start=j == 0, stop=False)
                        ins = pe.matmul(acc[h][:, :], sgn2T[:, j, :], hid_lo[:, j, cols], start=False, stop=j == NF - 1)
                    ins.then_inc(s_down, 1)

                def turn_qk(n):
                    h = n // 2
                    pe.wait_ge(s_rot_add, at(NG, q, h + 1))
                    pe.wait_ge(s_skip, at(NG, q, h + 1))
                    if n >= 2:
                        pe.wait_ge(s_qkT_lo, at(2 * NG, q, n - 1))
                    elif has_a:
                        wait_probT_read(1, KEYS[1] - 2 + n)
                    for t in range(TG):
                        ins = pe.transpose(turn[n % 2][:, t * P:(t + 1) * P],
                                           qk_tok[:, 2 * (TG * h + t) + n % 2, :], ident[:, :])
                    ins.then_inc(s_qkT, 1)

                def turn_y(h):
                    pe.wait_ge(s_y_out, at(NG, o, h + 1))
                    if has_q:
                        pe.wait_ge(s_xT_lo, at(NG, q, h + 1))
                    elif has_a:
                        wait_probT_read(0, KEYS[0] - 2 + h)
                    for t in range(TG):
                        me = slice((TG * h + t) * P, (TG * h + t + 1) * P)
                        ins = pe.transpose(turn[h][:, t * P:(t + 1) * P], yT[:, me], ident[:, :])
                    ins.then_inc(s_yT, 1)

                if has_a:
                    scores(0)
                    scores(1)
                if has_f:
                    for j in range(3):
                        weigh(1, j, f)
                if has_a:
                    scores(2)
                if has_f:
                    weigh(1, 3, f)
                if has_a:
                    scores(3)
                if has_f:
                    weigh(1, 4, f)
                    weigh(1, 5, f)
                if has_a:
                    scores(4)
                if has_f:
                    weigh(1, 6, f)
                    weigh(1, 7, f)
                if has_a:
                    scores(5)
                    turn_prob(0, 0)
                    turn_prob(0, 1)
                if has_o:
                    down(0)
                if has_f:
                    project_out(1, f)
                if has_a:
                    scores(6)
                if has_o:
                    down(1)
                if has_a:
                    turn_prob(0, 2)
                    turn_prob(0, 3)
                    scores(7)
                if has_q:
                    turn_x(0)
                    turn_x(1)
                if has_a:
                    for j in range(4):
                        weigh(0, j, a)
                if has_o:
                    turn_y(0)
                    turn_y(1)
                if has_q:
                    project_qk(0)
                if has_a:
                    turn_prob(1, 0)
                    turn_prob(1, 1)
                    project_out(0, a)
                if has_f:
                    turn_x1(0)
                    turn_x1(1)
                if has_q:
                    project_qk(1)
                if has_a:
                    turn_prob(1, 2)
                    turn_prob(1, 3)
                if has_f:
                    up(0)
                if has_a:
                    turn_prob(1, 4)
                    turn_prob(1, 5)
                if has_f:
                    up(1)
                if has_a:
                    turn_prob(1, 6)
                    turn_prob(1, 7)
                if has_q:
                    turn_qk(0)
                    turn_qk(1)
                if has_f:
                    up(2)
                    up(3)
                if has_q:
                    turn_qk(2)
                    turn_qk(3)

            run_steps(pe, step)

        @block.scalar
        def _(act):
            def step(b):
                has_q, has_a, has_f, has_o, has_z = stages(b)
                q, a, f, o, z = (b, 1), (b, 0), (b, -1), (b, -2), (b, -3)

                def exponentials(r):
                    if r == 0 and not (isinstance(b, int) and b == 0):
                        act.wait_ge(s_rinv, at(1, a, 0))
                    act.wait_ge(s_max, at(NT, a, r + 1))
                    act.activation(prob[:, ROW[r]:ROW[r + 1]], wide[r % 2][:, 0:(r + 1) * P], ACT.Exp,
                                   bias=negmax[:, r:r + 1], accum_out=rowsum[:, r:r + 1]).then_inc(s_exp, 1)

                def probT_out(g, j):
                    act.wait_ge(s_probT, at(NPT, a, slot_of_probT(g, j) + 1))
                    lo = max(j - TG * g, 0) * P
                    act.activation(probT[g][:, j, lo:BANK], turn[j % 2][:, lo:BANK], ACT.Copy).then_inc(s_probT_act, 1)

                def high_part(dst, src, ready, per, c, k, done):
                    act.wait_ge(ready, at(per, c, k))
                    act.activation(dst, src, ACT.Copy).then_inc(done, 1)

                def gelu(j):
                    act.wait_ge(s_up, at(NF, f, j + 1))
                    act.activation(hid[:, j, :], wide[j % 2][:, :], ACT.Gelu, bias=b1_sb[:, j:j + 1],
                                   scale=alpha1[:, j:j + 1]).then_inc(s_gelu, 1)

                def px_out(g, c):
                    act.wait_ge(s_px, at(NG, c, g + 1))
                    act.activation(pxT[:, g, :], acc[g][:, :], ACT.Copy).then_inc(s_px_out, 1)

                def halves(h):
                    return slice(h * BANK, (h + 1) * BANK)

                def y_out_half(h):
                    act.wait_ge(s_down, at(NG, o, h + 1))
                    act.activation(yT[:, halves(h)], acc[h][:, :], ACT.Identity, bias=b2_sb[:, 0:1],
                                   scale=alpha2[:, 0:1]).then_inc(s_y_out, 1)

                def skipped(h):
                    act.wait_ge(s_rot_mul, at(NG, q, h + 1))
                    act.activation(qk_tok[:, 2 * TG * h:2 * TG * (h + 1), ROT:D],
                                   wide[h][:, :].rearrange("p (n d) -> p n d", d=D)[:, :, ROT:D],
                                   ACT.Copy).then_inc(s_skip, 1)

                def qkT_high(n):
                    high_part(qkT_hi[:, n % 2, halves(n // 2)], turn[n % 2][:, :], s_qkT, 2 * NG, q, n + 1, s_qkT_hi)

                if has_a:
                    for r in range(5):
                        exponentials(r)
                if has_f:
                    px_out(1, f)
                if has_a:
                    exponentials(5)
                    probT_out(0, 0)
                    probT_out(0, 1)
                if has_o:
                    y_out_half(0)
                if has_a:
                    exponentials(6)
                if has_o:
                    y_out_half(1)
                if has_a:
                    probT_out(0, 2)
                    probT_out(0, 3)
                if has_q:
                    for h in range(NG):
                        high_part(xT_hi[:, halves(h)], turn[h][:, :], s_xT, NG, q, h + 1, s_xT_hi)
                if has_a:
                    exponentials(7)
                    px_out(0, a)
                    probT_out(1, 0)
                    probT_out(1, 1)
                if has_f:
                    for h in range(NG):
                        high_part(x1T_hi[:, halves(h)], turn[h][:, :], s_x1T, NG, f, h + 1, s_x1T_hi)
                if has_q:
                    skipped(0)
                if has_a:
                    probT_out(1, 2)
                    probT_out(1, 3)
                if has_q:
                    skipped(1)
                if has_f:
                    if isinstance(b, int) and b == 1:
                        act.wait_ge(s_weights, 1)
                    gelu(0)
                if has_f:
                    gelu(1)
                if has_q:
                    qkT_high(0)
                    qkT_high(1)
                if has_f:
                    gelu(2)
                    gelu(3)
                if has_q:
                    qkT_high(2)
                    qkT_high(3)

            run_steps(act, step)

        @block.vector
        def _(dve):
            dve.wait_ge(s_wqk_in, 32)
            dve.tensor_scalar(wqk[:, 0:D], wqk[:, 0:D], 1.0 / D, None, ALU.mult).then_inc(s_prep_dve, 1)
            dve.wait_ge(s_prep_dve, 1)
            dve.tensor_copy(wqk_hi[:, :], wqk[:, :]).then_inc(s_prep_dve, 1)
            dve.wait_ge(s_prep_dve, 2)
            dve.tensor_tensor(wqk_lo[:, :], wqk[:, :], wqk_hi[:, :].bitcast(F32), ALU.subtract).then_inc(s_prep_dve, 1)
            dve.wait_ge(s_w_in, 16 * 10)
            dve.tensor_scalar(neg1[:, :, :], w1_sb[:, :, :], 0.0, None, ALU.is_lt).then_inc(s_prep_dve, 1)
            dve.tensor_scalar(neg2[:, :], w2_sb[:, :], 0.0, None, ALU.is_lt).then_inc(s_prep_dve, 1)
            dve.wait_ge(s_prep_dve, 5)
            dve.scalar_tensor_tensor(sgn1[:, :, :], w1_sb[:, :, :], 0.0, neg1[:, :, :], ALU.is_gt, ALU.subtract).then_inc(s_prep, 1)
            dve.scalar_tensor_tensor(sgn2[:, :], w2_sb[:, :], 0.0, neg2[:, :], ALU.is_gt, ALU.subtract).then_inc(s_prep, 1)
            dve.wait_ge(s_prep_pe, 1)
            dve.tensor_copy(wvT[:, :], acc[0][:, 0:P]).then_inc(s_prep, 1)
            dve.tensor_reduce(sum1[:, :], w1_sb[:, :, :], axis=AX.X, op=ALU.add, apply_absolute_value=True).then_inc(s_prep_dve, 1)
            dve.tensor_reduce(sum2[:, :], w2_sb[:, :], axis=AX.X, op=ALU.add, apply_absolute_value=True).then_inc(s_prep_dve, 1)
            dve.wait_ge(s_prep_dve, 7)
            dve.tensor_scalar(alpha1[:, :], sum1[:, :], 1.0 / D, None, ALU.mult)
            dve.tensor_scalar(alpha2[:, :], sum2[:, :], 1.0 / H, None, ALU.mult)
            dve.wait_ge(s_prep_pe, 2)
            dve.tensor_copy(sgn1T[:, :, :].rearrange("p f m -> p (f m)"), turn[0][:, :])
            dve.wait_ge(s_prep_pe, 3)
            dve.tensor_copy(sgn2T[:, :, :].rearrange("p f m -> p (f m)"), turn[1][:, :])
            dve.wait_ge(s_prep_pe, 4)
            dve.tensor_copy(wvo[:, :], acc[1][:, 0:D]).then_inc(s_weights, 1)

            def step(b):
                has_q, has_a, has_f, has_o, has_z = stages(b)
                q, a, f, o, z = (b, 1), (b, 0), (b, -1), (b, -2), (b, -3)

                def halves(h):
                    return slice(h * BANK, (h + 1) * BANK)

                def row_max(r):
                    dve.wait_ge(s_score, at(NT, a, r + 1))
                    dve.tensor_reduce(negmax[:, r:r + 1], wide[r % 2][:, 0:(r + 1) * P], axis=AX.X, op=ALU.max,
                                      negate=True).then_inc(s_max, 1)

                def low_part(dst, src, high, ready, per, c, k, done):
                    dve.wait_ge(ready, at(per, c, k))
                    dve.tensor_tensor(dst, src, high.bitcast(F32), ALU.subtract).then_inc(done, 1)

                def probT_copy(g, j):
                    dve.wait_ge(s_probT, at(NPT, a, slot_of_probT(g, j) + 1))
                    lo = max(j - TG * g, 0) * P
                    dve.tensor_copy(probT[g][:, j, lo:BANK], turn[j % 2][:, lo:BANK]).then_inc(s_probT_dve, 1)

                def hidden_high(j, c):
                    dve.wait_ge(s_gelu, at(NF, c, j + 1))
                    dve.tensor_copy(hid_hi[:, j, :], hid[:, j, :]).then_inc(s_hid_hi, 1)

                def rotate(h):
                    rows = slice(2 * TG * h, 2 * TG * (h + 1))
                    pairs = wide[h][:, :].rearrange("p (n d) -> p n d", d=D)
                    cos_h = cos_sb[:, :, :, :].rearrange("p n j d -> p (n j) d")[:, rows, :]
                    sin_h = sin_sb[:, :, :, :].rearrange("p n j d -> p (n j) d")[:, rows, :]
                    dve.wait_ge(s_qk, at(NG, q, h + 1))
                    dve.tensor_tensor(rot_cos[:, rows, :], pairs[:, :, 0:ROT], cos_h, ALU.mult)
                    dve.tensor_tensor(rot_sin[:, rows, 0:HALF], pairs[:, :, HALF:ROT], sin_h[:, :, 0:HALF], ALU.mult)
                    dve.tensor_tensor(rot_sin[:, rows, HALF:ROT], pairs[:, :, 0:HALF], sin_h[:, :, HALF:ROT],
                                      ALU.mult).then_inc(s_rot_mul, 1)

                def residual1(g, c):
                    dve.wait_ge(s_proj, at(NG, c, g + 1))
                    dve.wait_ge(s_rinv, at(1, c, 1))
                    if g == 0 and has_f:
                        dve.wait_ge(s_x1, at(NG, f, NG))
                    for t in range(TG * g, TG * (g + 1)):
                        c = t - TG * g
                        dve.scalar_tensor_tensor(res1[:, t, :], acc[g][:, c * D:(c + 1) * D], rinv[:, t:t + 1],
                                                 xa[:, t, :], ALU.mult, ALU.add).then_inc(s_res1, 1)

                def residual2(h):
                    dve.wait_ge(s_yT, at(NG, o, h + 1))
                    if h == 0 and has_z:
                        dve.wait_ge(s_y, at(1, z, 1))
                    dve.tensor_tensor(res2[:, TG * h:TG * (h + 1), :],
                                      turn[h][:, :].rearrange("p (n d) -> p n d", d=D),
                                      x1[:, TG * h:TG * (h + 1), :], ALU.add).then_inc(s_res2, 1)

                def statistics(res, stat, ready, per, c, done):
                    dve.wait_ge(ready, at(per, c, per))
                    for t in range(NT):
                        ins = dve.bn_stats(stat[:, t, :], res[:, t, :])
                    ins.then_inc(done, 1)

                def normalize(dst, res, ln, t):
                    return dve.tensor_scalar(dst[:, t, :], res[:, t, :], ln[:, MEAN, t:t + 1],
                                             ln[:, RSTD, t:t + 1], ALU.subtract, ALU.mult)

                def qkT_low(n):
                    h, j = n // 2, n % 2
                    low_part(qkT_lo[:, j, halves(h)], turn[j][:, :], qkT_hi[:, j, halves(h)],
                             s_qkT_hi, 2 * NG, q, n + 1, s_qkT_lo)

                if has_o:
                    hidden_high(3, o)
                if has_a:
                    row_max(0)
                    row_max(1)
                if has_z:
                    statistics(res2, stat2, s_res2, NG, z, s_stat2)
                if has_a:
                    for r in range(2, 6):
                        row_max(r)
                if has_z:
                    dve.wait_ge(s_ln2, at(LN_STEPS, z, LN_STEPS))
                    if not (isinstance(b, int) and b == 3):
                        dve.wait_ge(s_stored, at(16, z, 0))
                    for t in range(NT):
                        ins = normalize(y_out, res2, ln2, t)
                    ins.then_inc(s_y, 1)
                if has_f:
                    residual1(1, f)
                if has_a:
                    row_max(6)
                if has_f:
                    statistics(res1, stat1, s_res1, NT, f, s_stat1)
                if has_a:
                    row_max(7)
                if has_q:
                    for h in range(NG):
                        low_part(xT_lo[:, halves(h)], turn[h][:, :], xT_hi[:, halves(h)], s_xT_hi, NG, q, h + 1, s_xT_lo)
                if has_o:
                    residual2(0)
                    residual2(1)
                if has_f:
                    dve.wait_ge(s_ln1, at(LN_STEPS, f, LN_STEPS))
                    if has_o:
                        dve.wait_ge(s_res2, at(NG, o, NG))
                    for h in range(NG):
                        for t in range(TG * h, TG * (h + 1)):
                            ins = normalize(x1, res1, ln1, t)
                        ins.then_inc(s_x1, 1)
                if has_a:
                    dve.wait_ge(s_exp, at(NT, a, NT))
                    if has_f:
                        dve.wait_ge(s_res1, at(NT, f, NT))
                    dve.reciprocal(rinv[:, :], rowsum[:, :]).then_inc(s_rinv, 1)
                if has_q:
                    rotate(0)
                if has_f:
                    for h in range(NG):
                        low_part(x1T_lo[:, halves(h)], turn[h][:, :], x1T_hi[:, halves(h)], s_x1T_hi, NG, f, h + 1, s_x1T_lo)
                if has_a:
                    residual1(0, a)
                if has_q:
                    rotate(1)
                if has_a:
                    for j in range(4, 8):
                        probT_copy(1, j)
                if has_f:
                    hidden_high(0, f)
                    hidden_high(1, f)
                if has_q:
                    qkT_low(0)
                    qkT_low(1)
                if has_f:
                    hidden_high(2, f)
                if has_q:
                    qkT_low(2)
                    qkT_low(3)

            run_steps(dve, step)


def rotation_tables(T, D, base=10000.0):
    half = D // 4
    freqs = np.power(np.float32(base), -np.arange(half, dtype=np.float32) / np.float32(half), dtype=np.float32)
    radians = np.arange(T, dtype=np.float32)[:, None] * freqs[None, :]
    cos, sin = np.cos(radians), np.sin(radians)
    return (np.concatenate([cos, cos], axis=1).astype(np.float32),
            np.concatenate([-sin, sin], axis=1).astype(np.float32))


_INS = ['L0_attn_x', 'L0_attn_wq', 'L0_attn_wk', 'L0_attn_wv', 'L0_attn_wo',
        'L0_ffn_w1', 'L0_ffn_b1', 'L0_ffn_w2', 'L0_ffn_b2']


def kernel(**inputs):
    import concourse.bacc as _bacc
    from concourse.bass_utils import run_bass_kernel_spmd as _run

    nc = _bacc.Bacc("TRN2", target_bir_lowering=False, num_devices=1)
    given = {name: np.ascontiguousarray(inputs[name]) for name in _INS}
    given["cos"], given["sin"] = rotation_tables(given['L0_attn_x'].shape[1], given['L0_attn_x'].shape[2])
    arrays, args = {}, []
    for name, a in given.items():
        arrays[f"in_{name}_dram"] = a
        args.append(nc.dram_tensor(f"in_{name}_dram", a.shape, mybir.dt.from_np(a.dtype), kind="ExternalInput").ap())
    shape = given['L0_attn_x'].shape
    args.append(nc.dram_tensor("out_0_dram", shape, F32, kind="ExternalOutput").ap())
    attention_ffn_kernel(nc, *args)
    r = _run(nc, [arrays], core_ids=[0])
    return r.results[0]["out_0_dram"]
```

```python
import numpy as np
import concourse.bass as bass
from concourse import mybir
from contextlib import ExitStack

F32 = mybir.dt.float32
F32R = mybir.dt.float32r
BF16 = mybir.dt.bfloat16
ALU = mybir.AluOpType
ACT = mybir.ActivationFunctionType
AX = mybir.AxisListType

LN_EPS = 1e-5
MASKED = -1e30


def attention_ffn_kernel(nc, x, wq, wk, wv, wo, w1, b1, w2, b2, cos_t, sin_t, out):
    B, T, D = x.shape
    H = w1.shape[0]
    P = 128
    NT = T // P
    NF = H // P
    BANK = 512
    TG = BANK // P
    NG = NT // TG
    ROT = D // 2
    HALF = ROT // 2
    ROW = [P * (r * (r + 1) // 2) for r in range(NT + 1)]
    KEYS = [TG * (g + 1) for g in range(NG)]
    NPT = sum(KEYS)
    ACT_PT = NPT - 4
    DVE_PT = NPT - ACT_PT
    LN_STEPS = 9
    FACTOR_STEPS = 7
    MEAN, MINUS_MEAN, SHIFT, VAR, RSTD = 2, 3, 6, 7, 8

    ctx = ExitStack()
    with ctx:
        def sb(name, shape, dt=F32):
            return ctx.enter_context(nc.sbuf_tensor(name, shape, dt))

        def sem(name):
            return ctx.enter_context(nc.semaphore(name))

        ident = sb("ident", [P, P])
        ident_bf = sb("ident_bf", [P, P], BF16)
        mask_bf = sb("mask_bf", [P, P], BF16)
        minus_half = sb("minus_half", [P, NT])
        halves_c = sb("halves_c", [P, 2, NT])
        inv_d_c = sb("inv_d_c", [P, NT])
        eps_c = sb("eps_c", [P, NT])
        cos_sb = sb("cos_sb", [P, NT, 2, ROT])
        sin_sb = sb("sin_sb", [P, NT, 2, ROT])
        wqk = sb("wqk", [P, 2 * D])
        wqk_hi = sb("wqk_hi", [P, 2 * D], F32R)
        wqk_lo = sb("wqk_lo", [P, 2 * D], F32R)
        wv_sb = sb("wv_sb", [P, D])
        wvT = sb("wvT", [P, D])
        wo_sb = sb("wo_sb", [P, D])
        wvo = sb("wvo", [P, D])
        w1_sb = sb("w1_sb", [P, NF, D])
        w2_sb = sb("w2_sb", [P, H])
        neg1 = sb("neg1", [P, NF, D])
        neg2 = sb("neg2", [P, H])
        sgn1 = sb("sgn1", [P, NF, D])
        sgn2 = sb("sgn2", [P, H])
        sgn1T = sb("sgn1T", [P, NF, P], F32R)
        sgn2T = sb("sgn2T", [P, NF, D], F32R)
        sum1 = sb("sum1", [P, NF])
        sum2 = sb("sum2", [P, 1])
        alpha1 = sb("alpha1", [P, NF])
        alpha2 = sb("alpha2", [P, 1])
        b1_sb = sb("b1_sb", [P, NF])
        b2_sb = sb("b2_sb", [P, 1])
        xq = sb("xq", [P, NT, D])
        xT_hi = sb("xT_hi", [P, T], F32R)
        xT_lo = sb("xT_lo", [P, T], F32R)
        rot_cos = sb("rot_cos", [P, NT * 2, ROT])
        rot_sin = sb("rot_sin", [P, NT * 2, ROT])
        qk_tok = sb("qk_tok", [P, NT * 2, D])
        qkT_hi = sb("qkT_hi", [P, 2, T], F32R)
        qkT_lo = sb("qkT_lo", [P, 2, T], F32R)
        xa = sb("xa", [P, NT, D])
        negmax = sb("negmax", [P, NT])
        rowsum = sb("rowsum", [P, NT])
        rinv = sb("rinv", [P, NT])
        prob = sb("prob", [P, ROW[NT]])
        probT = [sb(f"probT{g}", [P, KEYS[g], BANK]) for g in range(NG)]
        pxT = sb("pxT", [P, NG, BANK])
        res1 = sb("res1", [P, NT, D])
        stat1 = sb("stat1", [P, NT, 6])
        ln1 = sb("ln1", [P, LN_STEPS, NT])
        x1 = sb("x1", [P, NT, D])
        x1T_hi = sb("x1T_hi", [P, T], F32R)
        x1T_lo = sb("x1T_lo", [P, T], F32R)
        hid = sb("hid", [P, NF, T])
        hid_hi = sb("hid_hi", [P, NF, T], F32R)
        hid_lo = sb("hid_lo", [P, NF, T], F32R)
        yT = sb("yT", [P, T])
        res2 = sb("res2", [P, NT, D])
        stat2 = sb("stat2", [P, NT, 6])
        ln2 = sb("ln2", [P, LN_STEPS, NT])
        y_out = sb("y_out", [P, NT, D])

        wide = [ctx.enter_context(nc.psum_tensor(f"wide{i}", [P, 2 * BANK], F32)) for i in range(2)]
        turn = [ctx.enter_context(nc.psum_tensor(f"turn{i}", [P, BANK], F32)) for i in range(2)]
        acc = [ctx.enter_context(nc.psum_tensor(f"acc{i}", [P, BANK], F32)) for i in range(2)]

        s_wqk_in, s_table_in, s_w_in = sem("s_wqk_in"), sem("s_table_in"), sem("s_w_in")
        s_xq_in, s_xa_in, s_stored = sem("s_xq_in"), sem("s_xa_in"), sem("s_stored")
        s_const, s_prep, s_prep_pe, s_prep_dve, s_weights = (
            sem("s_const"), sem("s_prep"), sem("s_prep_pe"), sem("s_prep_dve"), sem("s_weights"))
        s_xT, s_qk, s_qkT = sem("s_xT"), sem("s_qk"), sem("s_qkT")
        s_score, s_probT, s_px, s_proj = sem("s_score"), sem("s_probT"), sem("s_px"), sem("s_proj")
        s_x1T, s_up, s_down, s_yT = sem("s_x1T"), sem("s_up"), sem("s_down"), sem("s_yT")
        s_xT_hi, s_skip, s_qkT_hi = sem("s_xT_hi"), sem("s_skip"), sem("s_qkT_hi")
        s_exp, s_probT_act, s_px_out = sem("s_exp"), sem("s_probT_act"), sem("s_px_out")
        s_x1T_hi, s_gelu, s_y_out = sem("s_x1T_hi"), sem("s_gelu"), sem("s_y_out")
        s_xT_lo, s_rot_mul, s_qkT_lo = sem("s_xT_lo"), sem("s_rot_mul"), sem("s_qkT_lo")
        s_max, s_rinv, s_res1, s_stat1, s_x1 = sem("s_max"), sem("s_rinv"), sem("s_res1"), sem("s_stat1"), sem("s_x1")
        s_probT_dve = sem("s_probT_dve")
        s_x1T_lo, s_hid_hi, s_res2, s_stat2, s_y = sem("s_x1T_lo"), sem("s_hid_hi"), sem("s_res2"), sem("s_stat2"), sem("s_y")
        s_rot_add, s_hid_lo, s_ln1, s_ln2 = sem("s_rot_add"), sem("s_hid_lo"), sem("s_ln1"), sem("s_ln2")
        s_hid_lo_dve, s_stats_tail, s_factors = sem("s_hid_lo_dve"), sem("s_stats_tail"), sem("s_factors")
        s_minus_mean, s_y_last = sem("s_minus_mean"), sem("s_y_last")
        s_rstd, s_shift = sem("s_rstd"), sem("s_shift")

        def at(per, c, k):
            return per * c[0] + (per * c[1] + k)

        def run_steps(eng, step):
            for b in range(-1, 4):
                step(b)
            with eng.Fori(4, B - 1) as b:
                step(b)
            step(B - 1)

        def halves(h):
            return slice(h * BANK, (h + 1) * BANK)

        def tiles(h):
            return range(TG * h, TG * (h + 1))

        end2, end1, end = (B - 3, 0), (B - 2, 0), (B - 1, 0)
        x1_last, res2_last, y_last = xq, res1, x1
        sums_end1 = [acc[0][:, :], wide[0][:, BANK:2 * BANK]]

        def stages(b):
            if not isinstance(b, int):
                return True, True, True, True, True
            return b < B - 1, b >= 0, b >= 1, b >= 2, b >= 3

        block = ctx.enter_context(nc.Block())

        @block.sync
        def _(sp):
            sp.dma_start(xq[:, :, :], x[0].rearrange("(n p) d -> p n d", p=P)).then_inc(s_xq_in, 16)
            sp.dma_start(wqk[:, 0:D], wq[0]).then_inc(s_wqk_in, 16)
            sp.dma_start(wqk[:, D:2 * D], wk[0]).then_inc(s_wqk_in, 16)
            sp.dma_start(cos_sb[:, :, :, :], cos_t).then_inc(s_table_in, 16)
            sp.dma_start(sin_sb[:, :, :, :], sin_t).then_inc(s_table_in, 16)
            sp.dma_start(wv_sb[:, :], wv[0]).then_inc(s_w_in, 16)
            sp.dma_start(wo_sb[:, :], wo).then_inc(s_w_in, 16)
            sp.dma_start(w1_sb[:, :, :], w1.rearrange("(p f) d -> p f d", f=NF)).then_inc(s_w_in, 16)
            sp.dma_start(w2_sb[:, :], w2).then_inc(s_w_in, 16)
            sp.dma_start(b1_sb[:, :], b1.rearrange("(p f) -> p f", f=NF)).then_inc(s_w_in, 16)
            sp.dma_start(b2_sb[:, :], b2.rearrange("(p a) -> p a", a=1)).then_inc(s_w_in, 16)

            def step(b):
                has_q, has_a, _, _, has_z = stages(b)
                if has_q and has_a:
                    sp.wait_ge(s_xT, at(NG, (b, 0), NG))
                    sp.dma_start(xq[:, :, :], x[b + 1].rearrange("(n p) d -> p n d", p=P)).then_inc(s_xq_in, 16)
                if has_a:
                    if not (isinstance(b, int) and b == 0):
                        sp.wait_ge(s_res1, at(NT, (b, 0), 0))
                    sp.dma_start(xa[:, :, :], x[b].rearrange("(n p) d -> p n d", p=P)).then_inc(s_xa_in, 16)
                if has_z:
                    sp.wait_ge(s_y, at(1, (b, -3), 1))
                    sp.dma_start(out[b - 3].rearrange("(n p) d -> p n d", p=P), y_out[:, :, :]).then_inc(s_stored, 16)

            run_steps(sp, step)
            sp.wait_ge(s_y, at(1, end2, 1))
            sp.dma_start(out[B - 3].rearrange("(n p) d -> p n d", p=P), y_out[:, :, :]).then_inc(s_stored, 16)
            for c, y, done, before in ((B - 2, y_out, s_y, B - 2), (B - 1, y_last, s_y_last, 0)):
                for h in range(NG):
                    sp.wait_ge(done, before + h + 1)
                    sp.dma_start(out[c][halves(h), :].rearrange("(n p) d -> p n d", p=P),
                                 y[:, TG * h:TG * (h + 1), :]).then_inc(s_stored, 16)
            sp.wait_ge(s_stored, 16 * (B - 2 + 2 * NG))

        @block.gpsimd
        def _(pool):
            pool.memset(ident[:, :], 0.0).then_inc(s_const, 1)
            pool.memset(ident_bf[:, :], 0.0).then_inc(s_const, 1)
            pool.memset(mask_bf[:, :], 0.0).then_inc(s_const, 1)
            for c, value in ((minus_half[:, :], -0.5), (halves_c[:, :, :], 0.5), (inv_d_c[:, :], 1.0 / D),
                             (eps_c[:, :], LN_EPS)):
                pool.memset(c, value).then_inc(s_const, 1)
            pool.wait_ge(s_const, 7)
            for m in (ident, ident_bf):
                pool.affine_select(out=m[:, :], in_=m[:, :], compare_op=ALU.not_equal, fill=1.0,
                                   base=0, pattern=[[-1, P]], channel_multiplier=1).then_inc(s_const, 1)
            pool.affine_select(out=mask_bf[:, :], in_=mask_bf[:, :], compare_op=ALU.is_ge, fill=MASKED,
                               base=0, pattern=[[-1, P]], channel_multiplier=1).then_inc(s_const, 1)

            def norm_factors(stat, ln, done, c):
                def after(n):
                    pool.wait_ge(done, at(LN_STEPS, c, n))

                mean_e, m2_e, mean_o, m2_o = (stat[:, :, j] for j in (1, 2, 4, 5))
                total, diff, mean, half, m2, part, half2, var, rstd = (ln[:, j, :] for j in range(LN_STEPS))
                pool.tensor_tensor(total, mean_e, mean_o, ALU.add).then_inc(done, 1)
                pool.tensor_tensor(diff, mean_e, mean_o, ALU.subtract).then_inc(done, 1)
                pool.tensor_tensor(m2, m2_e, m2_o, ALU.add).then_inc(done, 1)
                after(2)
                pool.tensor_tensor(ln[:, 2:4, :], ln[:, 0:2, :], halves_c[:, :, :], ALU.mult).then_inc(done, 1)
                after(3)
                pool.tensor_tensor(part, m2, inv_d_c[:, :], ALU.mult).then_inc(done, 1)
                after(4)
                pool.tensor_tensor(half2, half, half, ALU.mult).then_inc(done, 1)
                after(6)
                pool.tensor_tensor(var, part, half2, ALU.add).then_inc(done, 1)
                after(7)
                pool.tensor_tensor(var, var, eps_c[:, :], ALU.add).then_inc(done, 1)
                after(8)
                pool.tensor_tensor(rstd, var, minus_half[:, :], ALU.pow).then_inc(done, 1)

            def rstd(ln, h, n, k=1):
                pool.wait_ge(s_factors, FACTOR_STEPS * (n + 1))
                ts = slice(TG * h, TG * (h + k))
                pool.tensor_tensor(ln[:, RSTD, ts], ln[:, VAR, ts], minus_half[:, ts], ALU.pow).then_inc(s_rstd, 1)

            def step(b):
                has_q, has_a, has_f, has_o, has_z = stages(b)
                q, f, z = (b, 1), (b, -1), (b, -3)
                last = isinstance(b, int) and b == B - 1

                def first_factors():
                    pool.wait_ge(s_stat1, at(1, f, 1))
                    norm_factors(stat1, ln1, s_ln1, f)

                def second_factors(c):
                    pool.wait_ge(s_stat2, at(1, c, 1))
                    norm_factors(stat2, ln2, s_ln2, c)

                def rotation_sum(h):
                    rows = slice(2 * TG * h, 2 * TG * (h + 1))
                    pool.wait_ge(s_rot_mul, at(NG, q, h + 1))
                    pool.tensor_tensor(qk_tok[:, rows, 0:ROT], rot_cos[:, rows, :], rot_sin[:, rows, :],
                                       ALU.add).then_inc(s_rot_add, 1)

                def hidden_low(j):
                    if last and j % 2 == 1:
                        return
                    pool.wait_ge(s_hid_hi, at(NF, f, j + 1))
                    pool.tensor_tensor(hid_lo[:, j, :], hid[:, j, :], hid_hi[:, j, :].bitcast(F32),
                                       ALU.subtract).then_inc(s_hid_lo, 1)

                if has_z:
                    second_factors(z)
                if has_f:
                    first_factors()
                if last:
                    rstd(ln1, 0, 0)
                if has_q:
                    rotation_sum(0)
                    rotation_sum(1)
                if last:
                    second_factors(end2)
                if has_f:
                    hidden_low(0)
                    hidden_low(1)
                    hidden_low(2)
                    hidden_low(3)

            run_steps(pool, step)

            def hidden_low_half(h, j):
                pool.wait_ge(s_hid_hi, at(NF, end, NF * h + j + 1))
                pool.tensor_tensor(hid_lo[:, j, halves(h)], hid[:, j, halves(h)],
                                   hid_hi[:, j, halves(h)].bitcast(F32), ALU.subtract).then_inc(s_hid_lo, 1)

            def shift():
                pool.wait_ge(s_rstd, 3)
                pool.wait_ge(s_minus_mean, 1)
                pool.tensor_tensor(ln2[:, SHIFT, :], ln2[:, MINUS_MEAN, :], ln2[:, RSTD, :], ALU.mult).then_inc(s_shift, 1)

            rstd(ln1, 1, 1)
            hidden_low_half(0, 0)
            hidden_low_half(0, 2)
            hidden_low_half(1, 0)
            hidden_low_half(1, 2)
            rstd(ln2, 0, 2, NG)
            shift()
            rstd(ln1, 0, 3)
            rstd(ln1, 1, 4)

        def slot_of_probT(g, j):
            return sum(KEYS[:g]) + j

        @block.tensor
        def _(pe):
            pe.wait_ge(s_const, 10)

            def wait_probT_read(g, j, c):
                u = slot_of_probT(g, j)
                if u < ACT_PT:
                    pe.wait_ge(s_probT_act, at(ACT_PT, c, u + 1))
                else:
                    pe.wait_ge(s_probT_dve, at(DVE_PT, c, u + 1 - ACT_PT))

            def setup_turn_wv():
                pe.wait_ge(s_w_in, 16 * 6)
                pe.transpose(acc[1][:, 0:P], wv_sb[:, :], ident[:, :]).then_inc(s_prep_pe, 1)

            def setup_turn_sgn1():
                pe.wait_ge(s_prep, 1)
                for f in range(NF):
                    ins = pe.transpose(acc[0][:, f * P:(f + 1) * P], sgn1[:, f, :], ident[:, :])
                ins.then_inc(s_prep_pe, 1)

            def setup_wvo():
                pe.wait_ge(s_prep, 2)
                pe.matmul(acc[1][:, P:P + D], wvT[:, :], wo_sb[:, :], start=True, stop=True).then_inc(s_prep_pe, 1)

            def setup_turn_sgn2():
                pe.wait_ge(s_prep, 4)
                blocks = sgn2[:, :].rearrange("d (p f) -> d f p", f=NF)
                for f in range(NF):
                    ins = pe.transpose(acc[1][:, f * P:(f + 1) * P], blocks[:, f, :], ident[:, :])
                ins.then_inc(s_prep_pe, 1)

            def step(b):
                has_q, has_a, has_f, has_o, has_z = stages(b)
                q, a, f, o, z = (b, 1), (b, 0), (b, -1), (b, -2), (b, -3)
                early = isinstance(b, int) and b == -1
                setup = isinstance(b, int) and b == 0
                last = isinstance(b, int) and b == B - 1

                def scores(r):
                    n = 1 if r < TG else 2
                    if r in (0, TG):
                        pe.wait_ge(s_qkT_hi, at(2 * NG, a, 2 * n))
                        pe.wait_ge(s_qkT_lo, at(2 * NG, a, 2 * n))
                    if r >= 2:
                        pe.wait_ge(s_exp, at(NT, a, r - 1))
                    elif has_o:
                        pe.wait_ge(s_gelu, at(NF, o, 3 + r))
                    me = slice(r * P, (r + 1) * P)
                    parts = [(qkT_hi, qkT_hi), (qkT_hi, qkT_lo), (qkT_lo, qkT_hi)]
                    for lo in range(0, (r + 1) * P, BANK):
                        hi = min(lo + BANK, (r + 1) * P)
                        diagonal = hi == (r + 1) * P
                        for n, (qp, kp) in enumerate(parts):
                            ins = pe.matmul(wide[r % 2][:, lo:hi], qp[:, 0, me], kp[:, 1, lo:hi],
                                            start=n == 0, stop=n == 2 and not diagonal)
                        if diagonal:
                            ins = pe.matmul(wide[r % 2][:, hi - P:hi], ident_bf[:, :], mask_bf[:, :],
                                            start=False, stop=True)
                    ins.then_inc(s_score, 1)

                def turn_x1(h):
                    pe.wait_ge(s_x1, at(NG, f, h + 1))
                    wait_probT_read(1, h, a)
                    for t in range(TG):
                        ins = pe.transpose(turn[h][:, t * P:(t + 1) * P], x1[:, TG * h + t, :], ident[:, :])
                    ins.then_inc(s_x1T, 1)

                def turn_prob(g, j):
                    pe.wait_ge(s_exp, at(NT, a, TG * (g + 1)))
                    if g == 1 and j in (0, 1) and has_o:
                        pe.wait_ge(s_res2, at(NG, o, j + 1))
                    elif g == 1 and j in (0, 1):
                        pe.wait_ge(s_xT_lo, at(NG, q, j + 1))
                    elif g == 1 and j in (2, 3) and has_f:
                        pe.wait_ge(s_x1T_lo, at(NG, f, j - 1))
                    elif j >= 2:
                        wait_probT_read(g, j - 2, a)
                    for i in range(max(j, TG * g), TG * (g + 1)):
                        c = i - TG * g
                        ins = pe.transpose(turn[j % 2][:, c * P:(c + 1) * P],
                                           prob[:, ROW[i] + j * P:ROW[i] + (j + 1) * P], ident[:, :])
                    ins.then_inc(s_probT, 1)

                def weigh(g, j, c):
                    if g == 0 and j == 0:
                        if isinstance(b, int) and b == 0:
                            pe.wait_ge(s_weights, 1)
                        pe.wait_ge(s_xa_in, at(16, c, 16))
                        if has_o:
                            pe.wait_ge(s_y_out, at(NG, o, 1))
                    wait_probT_read(g, j, c)
                    lo = max(j - TG * g, 0) * P
                    ins = pe.matmul(acc[g][:, lo:BANK], xa[:, j, :], probT[g][:, j, lo:BANK],
                                    start=j == 0, stop=j == KEYS[g] - 1)
                    if j == KEYS[g] - 1:
                        ins.then_inc(s_px, 1)

                def project_out(g, c):
                    pe.wait_ge(s_px_out, at(NG, c, g + 1))
                    for t in range(TG):
                        ins = pe.matmul(acc[g][:, t * D:(t + 1) * D], pxT[:, g, t * P:(t + 1) * P], wvo[:, :],
                                        start=True, stop=True)
                    ins.then_inc(s_proj, 1)

                def turn_x(h):
                    pe.wait_ge(s_xq_in, at(16, q, 16))
                    if has_a:
                        wait_probT_read(0, KEYS[0] - 2 + h, a)
                    for t in range(TG):
                        ins = pe.transpose(turn[h][:, t * P:(t + 1) * P], xq[:, TG * h + t, :], ident[:, :])
                    ins.then_inc(s_xT, 1)

                def up(j):
                    if j == 0:
                        pe.wait_ge(s_x1T_hi, at(NG, f, NG))
                        pe.wait_ge(s_x1T_lo, at(NG, f, NG))
                    if j >= 2:
                        pe.wait_ge(s_gelu, at(NF, f, j - 1))
                    elif has_q:
                        pe.wait_ge(s_rot_mul, at(NG, q, j + 1))
                        pe.wait_ge(s_skip, at(NG, q, j + 1))
                    else:
                        pe.wait_ge(s_exp, at(NT, a, NT - 1 + j))
                    for h in range(NG):
                        cols = slice(h * BANK, (h + 1) * BANK)
                        pe.matmul(wide[j % 2][:, cols], sgn1T[:, j, :], x1T_hi[:, cols], start=True, stop=False)
                        ins = pe.matmul(wide[j % 2][:, cols], sgn1T[:, j, :], x1T_lo[:, cols], start=False, stop=True)
                    ins.then_inc(s_up, 1)

                def project_qk(h):
                    pe.wait_ge(s_xT_hi, at(NG, q, h + 1))
                    pe.wait_ge(s_xT_lo, at(NG, q, h + 1))
                    if has_a:
                        pe.wait_ge(s_exp, at(NT, a, NT - 1 + h))
                    for t in range(TG):
                        me = slice((TG * h + t) * P, (TG * h + t + 1) * P)
                        cols = slice(t * 2 * D, (t + 1) * 2 * D)
                        pe.matmul(wide[h][:, cols], xT_hi[:, me], wqk_hi[:, :], start=True, stop=False)
                        pe.matmul(wide[h][:, cols], xT_hi[:, me], wqk_lo[:, :], start=False, stop=False)
                        ins = pe.matmul(wide[h][:, cols], xT_lo[:, me], wqk_hi[:, :], start=False, stop=True)
                    ins.then_inc(s_qk, 1)

                def down(h):
                    pe.wait_ge(s_res1, at(NT, f, TG * (h + 1)))
                    cols = slice(h * BANK, (h + 1) * BANK)
                    for j in range(NF):
                        pe.wait_ge(s_hid_hi, at(NF, o, j + 1))
                        pe.wait_ge(s_hid_lo, at(NF, o, j + 1))
                        pe.matmul(acc[h][:, :], sgn2T[:, j, :], hid_hi[:, j, cols], start=j == 0, stop=False)
                        ins = pe.matmul(acc[h][:, :], sgn2T[:, j, :], hid_lo[:, j, cols], start=False, stop=j == NF - 1)
                    ins.then_inc(s_down, 1)

                def turn_qk(n):
                    h = n // 2
                    pe.wait_ge(s_rot_add, at(NG, q, h + 1))
                    pe.wait_ge(s_skip, at(NG, q, h + 1))
                    if n >= 2:
                        pe.wait_ge(s_qkT_lo, at(2 * NG, q, n - 1))
                    elif has_a:
                        wait_probT_read(1, KEYS[1] - 2 + n, a)
                    for t in range(TG):
                        ins = pe.transpose(turn[n % 2][:, t * P:(t + 1) * P],
                                           qk_tok[:, 2 * (TG * h + t) + n % 2, :], ident[:, :])
                    ins.then_inc(s_qkT, 1)

                def turn_y(h):
                    pe.wait_ge(s_y_out, at(NG, o, h + 1))
                    if has_q:
                        pe.wait_ge(s_xT_lo, at(NG, q, h + 1))
                    else:
                        wait_probT_read(0, KEYS[0] - 2 + h, a)
                    for t in range(TG):
                        me = slice((TG * h + t) * P, (TG * h + t + 1) * P)
                        ins = pe.transpose(turn[h][:, t * P:(t + 1) * P], yT[:, me], ident[:, :])
                    ins.then_inc(s_yT, 1)

                if isinstance(b, int) and b <= 0:
                    if has_a:
                        scores(0)
                        scores(1)
                        scores(2)
                        scores(3)
                    if setup:
                        setup_wvo()
                    if has_a:
                        scores(4)
                        scores(5)
                        turn_prob(0, 0)
                        turn_prob(0, 1)
                    if setup:
                        setup_turn_sgn2()
                    if has_a:
                        scores(6)
                        turn_prob(0, 2)
                        turn_prob(0, 3)
                        scores(7)
                    if has_q:
                        turn_x(0)
                        turn_x(1)
                    if has_a:
                        weigh(0, 0, a)
                        weigh(0, 1, a)
                    if has_q:
                        project_qk(0)
                    if has_a:
                        weigh(0, 2, a)
                        turn_prob(1, 0)
                        weigh(0, 3, a)
                    if has_q:
                        project_qk(1)
                    if has_a:
                        turn_prob(1, 1)
                        turn_prob(1, 2)
                        project_out(0, a)
                    if early:
                        setup_turn_wv()
                    if has_a:
                        turn_prob(1, 3)
                        turn_prob(1, 4)
                        turn_prob(1, 5)
                        turn_prob(1, 6)
                        turn_prob(1, 7)
                    if has_q:
                        turn_qk(0)
                        turn_qk(1)
                    if early:
                        setup_turn_sgn1()
                    if has_q:
                        turn_qk(2)
                        turn_qk(3)
                    return

                if has_f:
                    weigh(1, 0, f)
                if has_a:
                    scores(0)
                if has_f:
                    weigh(1, 1, f)
                if has_a:
                    scores(1)
                if has_f:
                    weigh(1, 2, f)
                    weigh(1, 3, f)
                if has_a:
                    scores(2)
                    scores(3)
                if has_f:
                    weigh(1, 4, f)
                    weigh(1, 5, f)
                    weigh(1, 6, f)
                    weigh(1, 7, f)
                if has_a:
                    scores(4)
                    turn_prob(0, 0)
                if has_o:
                    down(0)
                if has_a:
                    scores(5)
                if has_f:
                    project_out(1, f)
                if has_a:
                    scores(6)
                    turn_prob(0, 1)
                if has_o:
                    down(1)
                if has_a:
                    turn_prob(0, 2)
                    turn_prob(0, 3)
                    scores(7)
                if has_q:
                    turn_x(0)
                    turn_x(1)
                if has_a:
                    weigh(0, 0, a)
                    weigh(0, 1, a)
                if has_o:
                    turn_y(0)
                    turn_y(1)
                if has_a:
                    weigh(0, 2, a)
                    weigh(0, 3, a)
                if has_q:
                    project_qk(0)
                if has_a:
                    turn_prob(1, 0)
                    turn_prob(1, 1)
                    project_out(0, a)
                if has_f:
                    turn_x1(0)
                    turn_x1(1)
                if has_q:
                    project_qk(1)
                if has_a:
                    turn_prob(1, 2)
                    turn_prob(1, 3)
                if has_f:
                    up(0)
                if has_a:
                    turn_prob(1, 4)
                    turn_prob(1, 5)
                if has_f:
                    up(1)
                if has_a:
                    turn_prob(1, 6)
                    turn_prob(1, 7)
                if has_q:
                    turn_qk(0)
                    turn_qk(1)
                if has_f:
                    up(2)
                    up(3)
                if has_q:
                    turn_qk(2)
                    turn_qk(3)

            run_steps(pe, step)

            def weigh(j):
                wait_probT_read(1, j, end)
                lo = max(j - TG, 0) * P
                ins = pe.matmul(acc[1][:, lo:BANK], xa[:, j, :], probT[1][:, j, lo:BANK],
                                start=j == 0, stop=j == KEYS[1] - 1)
                if j == KEYS[1] - 1:
                    ins.then_inc(s_px, 1)

            def project_out():
                pe.wait_ge(s_px_out, at(NG, end, 2))
                for t in range(TG):
                    ins = pe.matmul(acc[1][:, t * D:(t + 1) * D], pxT[:, 1, t * P:(t + 1) * P], wvo[:, :],
                                    start=True, stop=True)
                ins.then_inc(s_proj, 1)

            def down_block(j, h, dst, n):
                if j % 2 == 0:
                    pe.wait_ge(s_hid_lo, at(NF, end1, n))
                else:
                    pe.wait_ge(s_hid_lo_dve, n)
                pe.matmul(dst, sgn2T[:, j, :], hid_hi[:, j, halves(h)], start=j == 0, stop=False)
                ins = pe.matmul(dst, sgn2T[:, j, :], hid_lo[:, j, halves(h)], start=False, stop=j == NF - 1)
                if j == NF - 1:
                    ins.then_inc(s_down, 1)

            def down_prev(j):
                if j == 0:
                    pe.wait_ge(s_res1, at(NT, end, TG))
                    pe.wait_ge(s_gelu, at(NF, end1, 3))
                for h in range(NG):
                    down_block(j, h, sums_end1[h], j // 2 + 1)

            def down(h, j):
                if j == 0:
                    pe.wait_ge(s_res1, at(NT, end, TG * (h + 1)))
                    pe.wait_ge(s_y_out, at(NG, end1, NG))
                down_block(j, h, acc[h][:, :], 2 * (h + 1) + j // 2 + 1)

            def turn_y(h, c, read, count):
                pe.wait_ge(read, count)
                pe.wait_ge(s_y_out, at(NG, c, h + 1))
                for t in range(TG):
                    me = slice((TG * h + t) * P, (TG * h + t + 1) * P)
                    ins = pe.transpose(turn[h][:, t * P:(t + 1) * P], yT[:, me], ident[:, :])
                ins.then_inc(s_yT, 1)

            def turn_x1(h):
                wait_probT_read(1, NT - 2 + h, end)
                pe.wait_ge(s_x1, at(NG, end, h + 1))
                for t in range(TG):
                    ins = pe.transpose(turn[h][:, t * P:(t + 1) * P], x1_last[:, TG * h + t, :], ident[:, :])
                ins.then_inc(s_x1T, 1)

            def up(h, j):
                if j == 0:
                    pe.wait_ge(s_x1T_hi, at(NG, end, h + 1))
                    pe.wait_ge(s_x1T_lo, at(NG, end, h + 1))
                if h > 0:
                    pe.wait_ge(s_gelu, at(NF, end, j + 1))
                elif j == 1:
                    pe.wait_ge(s_gelu, at(NF, end1, NF))
                elif j == 2:
                    pe.wait_ge(s_y_out, at(NG, end1, NG))
                bank = wide[j % 2][:, halves(j // 2)]
                pe.matmul(bank, sgn1T[:, j, :], x1T_hi[:, halves(h)], start=True, stop=False)
                pe.matmul(bank, sgn1T[:, j, :], x1T_lo[:, halves(h)], start=False, stop=True).then_inc(s_up, 1)

            weigh(0)
            weigh(1)
            weigh(2)
            weigh(3)
            weigh(4)
            weigh(5)
            weigh(6)
            weigh(7)
            turn_x1(0)
            project_out()
            down_prev(0)
            down_prev(1)
            down_prev(2)
            down_prev(3)
            up(0, 0)
            up(0, 1)
            up(0, 2)
            turn_y(0, end1, s_x1T_lo, at(NG, end, 1))
            turn_x1(1)
            up(0, 3)
            up(1, 0)
            turn_y(1, end1, s_x1T_lo, at(NG, end, 2))
            up(1, 1)
            up(1, 2)
            up(1, 3)
            down(0, 0)
            down(0, 1)
            down(0, 2)
            down(0, 3)
            down(1, 0)
            down(1, 1)
            down(1, 2)
            down(1, 3)
            turn_y(0, end, s_res2, at(NG, end1, 1))
            turn_y(1, end, s_res2, at(NG, end1, 2))

        @block.scalar
        def _(act):
            def step(b):
                has_q, has_a, has_f, has_o, has_z = stages(b)
                q, a, f, o, z = (b, 1), (b, 0), (b, -1), (b, -2), (b, -3)
                last = isinstance(b, int) and b == B - 1

                def exponentials(r):
                    if r == 0 and not (isinstance(b, int) and b == 0):
                        act.wait_ge(s_rinv, at(1, a, 0))
                    act.wait_ge(s_max, at(NT, a, r + 1))
                    act.activation(prob[:, ROW[r]:ROW[r + 1]], wide[r % 2][:, 0:(r + 1) * P], ACT.Exp,
                                   bias=negmax[:, r:r + 1], accum_out=rowsum[:, r:r + 1]).then_inc(s_exp, 1)

                def probT_out(g, j):
                    act.wait_ge(s_probT, at(NPT, a, slot_of_probT(g, j) + 1))
                    lo = max(j - TG * g, 0) * P
                    act.activation(probT[g][:, j, lo:BANK], turn[j % 2][:, lo:BANK], ACT.Copy).then_inc(s_probT_act, 1)

                def high_part(dst, src, ready, per, c, k, done):
                    act.wait_ge(ready, at(per, c, k))
                    act.activation(dst, src, ACT.Copy).then_inc(done, 1)

                def gelu(j):
                    if isinstance(b, int) and b == 1 and j == 0:
                        act.wait_ge(s_weights, 1)
                    act.wait_ge(s_up, at(NF, f, j + 1))
                    act.activation(hid[:, j, :], wide[j % 2][:, :], ACT.Gelu, bias=b1_sb[:, j:j + 1],
                                   scale=alpha1[:, j:j + 1]).then_inc(s_gelu, 1)

                def px_out(g, c):
                    act.wait_ge(s_px, at(NG, c, g + 1))
                    act.activation(pxT[:, g, :], acc[g][:, :], ACT.Copy).then_inc(s_px_out, 1)

                def y_out_half(h):
                    act.wait_ge(s_down, at(NG, o, h + 1))
                    act.activation(yT[:, halves(h)], acc[h][:, :], ACT.Identity, bias=b2_sb[:, 0:1],
                                   scale=alpha2[:, 0:1]).then_inc(s_y_out, 1)

                def skipped(h):
                    act.wait_ge(s_rot_mul, at(NG, q, h + 1))
                    act.activation(qk_tok[:, 2 * TG * h:2 * TG * (h + 1), ROT:D],
                                   wide[h][:, :].rearrange("p (n d) -> p n d", d=D)[:, :, ROT:D],
                                   ACT.Copy).then_inc(s_skip, 1)

                def xT_high(h):
                    high_part(xT_hi[:, halves(h)], turn[h][:, :], s_xT, NG, q, h + 1, s_xT_hi)

                def x1T_high(h):
                    high_part(x1T_hi[:, halves(h)], turn[h][:, :], s_x1T, NG, f, h + 1, s_x1T_hi)

                def qkT_high(n):
                    high_part(qkT_hi[:, n % 2, halves(n // 2)], turn[n % 2][:, :], s_qkT, 2 * NG, q, n + 1, s_qkT_hi)

                if isinstance(b, int) and b <= 0:
                    if has_a:
                        exponentials(0)
                        exponentials(1)
                        exponentials(2)
                        exponentials(3)
                        exponentials(4)
                        probT_out(0, 0)
                        probT_out(0, 1)
                        exponentials(5)
                        probT_out(0, 2)
                        probT_out(0, 3)
                    if has_q:
                        xT_high(0)
                    if has_a:
                        exponentials(6)
                    if has_q:
                        xT_high(1)
                    if has_a:
                        exponentials(7)
                        probT_out(1, 0)
                        px_out(0, a)
                        probT_out(1, 1)
                        probT_out(1, 2)
                    if has_q:
                        skipped(0)
                    if has_a:
                        probT_out(1, 3)
                    if has_q:
                        skipped(1)
                        qkT_high(0)
                        qkT_high(1)
                        qkT_high(2)
                        qkT_high(3)
                    return

                if has_a:
                    exponentials(0)
                    exponentials(1)
                    exponentials(2)
                    exponentials(3)
                if has_f:
                    px_out(1, f)
                if has_a:
                    exponentials(4)
                    exponentials(5)
                    probT_out(0, 0)
                    probT_out(0, 1)
                    probT_out(0, 2)
                if has_o:
                    y_out_half(0)
                if has_a:
                    probT_out(0, 3)
                if has_q:
                    xT_high(0)
                    xT_high(1)
                if has_o:
                    y_out_half(1)
                if has_a:
                    exponentials(6)
                    exponentials(7)
                    px_out(0, a)
                    probT_out(1, 0)
                    probT_out(1, 1)
                if has_f:
                    x1T_high(0)
                    x1T_high(1)
                if has_q:
                    skipped(0)
                if has_a:
                    probT_out(1, 2)
                    probT_out(1, 3)
                if has_q:
                    skipped(1)
                if has_f:
                    gelu(0)
                    gelu(1)
                if has_q:
                    qkT_high(0)
                    qkT_high(1)
                if has_f:
                    gelu(2)
                if has_q:
                    qkT_high(2)
                    qkT_high(3)
                if has_f:
                    gelu(3)

            run_steps(act, step)

            def y_out_half(h, src, c):
                act.wait_ge(s_down, at(NG, c, h + 1))
                if c == end:
                    act.wait_ge(s_yT, at(NG, end1, h + 1))
                act.activation(yT[:, halves(h)], src, ACT.Identity, bias=b2_sb[:, 0:1],
                               scale=alpha2[:, 0:1]).then_inc(s_y_out, 1)

            def x1T_high(h):
                act.wait_ge(s_x1T, at(NG, end, h + 1))
                act.activation(x1T_hi[:, halves(h)], turn[h][:, :], ACT.Copy).then_inc(s_x1T_hi, 1)

            def gelu(h, j):
                act.wait_ge(s_up, at(NF, end, NF * h + j + 1))
                act.activation(hid[:, j, halves(h)], wide[j % 2][:, halves(j // 2)], ACT.Gelu,
                               bias=b1_sb[:, j:j + 1], scale=alpha1[:, j:j + 1]).then_inc(s_gelu, 1)

            def px_out():
                act.wait_ge(s_px, at(NG, end, 2))
                act.activation(pxT[:, 1, :], acc[1][:, :], ACT.Copy).then_inc(s_px_out, 1)

            def second_norm(h):
                if h == 0:
                    act.wait_ge(s_shift, 1)
                    act.wait_ge(s_stored, at(16, end1, 0))
                for t in tiles(h):
                    ins = act.activation(y_out[:, t, :], res2[:, t, :], ACT.Identity,
                                         bias=ln2[:, SHIFT, t:t + 1], scale=ln2[:, RSTD, t:t + 1])
                ins.then_inc(s_y, 1)

            px_out()
            x1T_high(0)
            y_out_half(0, sums_end1[0], end1)
            y_out_half(1, sums_end1[1], end1)
            gelu(0, 0)
            gelu(0, 1)
            gelu(0, 2)
            x1T_high(1)
            gelu(0, 3)
            gelu(1, 0)
            gelu(1, 1)
            gelu(1, 2)
            gelu(1, 3)
            y_out_half(0, acc[0][:, :], end)
            y_out_half(1, acc[1][:, :], end)
            second_norm(0)
            second_norm(1)

        @block.vector
        def _(dve):
            dve.wait_ge(s_wqk_in, 32)
            dve.tensor_scalar(wqk[:, 0:D], wqk[:, 0:D], 1.0 / D, None, ALU.mult).then_inc(s_prep_dve, 1)
            dve.wait_ge(s_prep_dve, 1)
            dve.tensor_copy(wqk_hi[:, :], wqk[:, :]).then_inc(s_prep_dve, 1)
            dve.wait_ge(s_prep_dve, 2)
            dve.tensor_tensor(wqk_lo[:, :], wqk[:, :], wqk_hi[:, :].bitcast(F32), ALU.subtract).then_inc(s_prep_dve, 1)

            def setup_signs1():
                dve.wait_ge(s_w_in, 16 * 6)
                dve.tensor_scalar(neg1[:, :, :], w1_sb[:, :, :], 0.0, None, ALU.is_lt).then_inc(s_prep_dve, 1)
                dve.tensor_scalar(neg2[:, :], w2_sb[:, :], 0.0, None, ALU.is_lt).then_inc(s_prep_dve, 1)
                dve.wait_ge(s_prep_dve, 5)
                dve.scalar_tensor_tensor(sgn1[:, :, :], w1_sb[:, :, :], 0.0, neg1[:, :, :], ALU.is_gt,
                                         ALU.subtract).then_inc(s_prep, 1)

            def setup_wvT():
                dve.wait_ge(s_prep_pe, 1)
                dve.tensor_copy(wvT[:, :], acc[1][:, 0:P]).then_inc(s_prep, 1)

            def setup_signs2():
                dve.scalar_tensor_tensor(sgn2[:, :], w2_sb[:, :], 0.0, neg2[:, :], ALU.is_gt,
                                         ALU.subtract).then_inc(s_prep, 1)
                dve.wait_ge(s_prep_pe, 2)
                dve.tensor_copy(sgn1T[:, :, :].rearrange("p f m -> p (f m)"), acc[0][:, :])

            def setup_wvo():
                dve.wait_ge(s_prep_pe, 3)
                dve.tensor_copy(wvo[:, :], acc[1][:, P:P + D]).then_inc(s_prep, 1)

            def setup_magnitudes():
                dve.tensor_reduce(sum1[:, :], w1_sb[:, :, :], axis=AX.X, op=ALU.add,
                                  apply_absolute_value=True).then_inc(s_prep_dve, 1)
                dve.tensor_reduce(sum2[:, :], w2_sb[:, :], axis=AX.X, op=ALU.add,
                                  apply_absolute_value=True).then_inc(s_prep_dve, 1)

            def setup_last():
                dve.wait_ge(s_prep_dve, 7)
                dve.tensor_scalar(alpha1[:, :], sum1[:, :], 1.0 / D, None, ALU.mult)
                dve.tensor_scalar(alpha2[:, :], sum2[:, :], 1.0 / H, None, ALU.mult)
                dve.wait_ge(s_prep_pe, 4)
                dve.tensor_copy(sgn2T[:, :, :].rearrange("p f m -> p (f m)"), acc[1][:, :]).then_inc(s_weights, 1)

            def statistics_tail(stat, res, h):
                for t in tiles(h):
                    ins = dve.bn_stats(stat[:, t, :], res[:, t, :])
                ins.then_inc(s_stats_tail, 1)

            def factors(stat, ln, h, n, k=1):
                ts = slice(TG * h, TG * (h + k))

                def after(i):
                    dve.wait_ge(s_factors, FACTOR_STEPS * n + i)

                dve.wait_ge(s_stats_tail, n + 1)
                mean_e, m2_e, mean_o, m2_o = (stat[:, ts, j] for j in (1, 2, 4, 5))
                total, diff, mean, _, m2, square, _, var, _ = (ln[:, j, ts] for j in range(LN_STEPS))
                dve.tensor_tensor(total, mean_e, mean_o, ALU.add).then_inc(s_factors, 1)
                dve.tensor_tensor(diff, mean_e, mean_o, ALU.subtract).then_inc(s_factors, 1)
                dve.tensor_tensor(m2, m2_e, m2_o, ALU.add).then_inc(s_factors, 1)
                after(1)
                dve.tensor_scalar(mean, total, 0.5, None, ALU.mult).then_inc(s_factors, 1)
                after(2)
                dve.scalar_tensor_tensor(square, diff, 0.25, diff, ALU.mult, ALU.mult).then_inc(s_factors, 1)
                after(5)
                dve.scalar_tensor_tensor(var, m2, 1.0 / D, square, ALU.mult, ALU.add).then_inc(s_factors, 1)
                after(6)
                dve.tensor_scalar(var, var, LN_EPS, None, ALU.add).then_inc(s_factors, 1)

            def hidden_low(j, n, cols=slice(0, T)):
                dve.wait_ge(s_hid_hi, at(NF, end1, n))
                dve.tensor_tensor(hid_lo[:, j, cols], hid[:, j, cols], hid_hi[:, j, cols].bitcast(F32),
                                  ALU.subtract).then_inc(s_hid_lo_dve, 1)

            def step(b):
                has_q, has_a, has_f, has_o, has_z = stages(b)
                q, a, f, o, z = (b, 1), (b, 0), (b, -1), (b, -2), (b, -3)
                early = isinstance(b, int) and b == -1
                setup = isinstance(b, int) and b == 0
                last = isinstance(b, int) and b == B - 1

                def row_max(r):
                    dve.wait_ge(s_score, at(NT, a, r + 1))
                    dve.tensor_reduce(negmax[:, r:r + 1], wide[r % 2][:, 0:(r + 1) * P], axis=AX.X, op=ALU.max,
                                      negate=True).then_inc(s_max, 1)

                def low_part(dst, src, high, ready, per, c, k, done):
                    dve.wait_ge(ready, at(per, c, k))
                    dve.tensor_tensor(dst, src, high.bitcast(F32), ALU.subtract).then_inc(done, 1)

                def probT_copy(g, j):
                    dve.wait_ge(s_probT, at(NPT, a, slot_of_probT(g, j) + 1))
                    lo = max(j - TG * g, 0) * P
                    dve.tensor_copy(probT[g][:, j, lo:BANK], turn[j % 2][:, lo:BANK]).then_inc(s_probT_dve, 1)

                def hidden_high(j, c):
                    dve.wait_ge(s_gelu, at(NF, c, j + 1))
                    dve.tensor_copy(hid_hi[:, j, :], hid[:, j, :]).then_inc(s_hid_hi, 1)

                def rotate(h):
                    rows = slice(2 * TG * h, 2 * TG * (h + 1))
                    pairs = wide[h][:, :].rearrange("p (n d) -> p n d", d=D)
                    cos_h = cos_sb[:, :, :, :].rearrange("p n j d -> p (n j) d")[:, rows, :]
                    sin_h = sin_sb[:, :, :, :].rearrange("p n j d -> p (n j) d")[:, rows, :]
                    if isinstance(b, int) and b == -1 and h == 0:
                        dve.wait_ge(s_table_in, 32)
                    dve.wait_ge(s_qk, at(NG, q, h + 1))
                    dve.tensor_tensor(rot_cos[:, rows, :], pairs[:, :, 0:ROT], cos_h, ALU.mult)
                    dve.tensor_tensor(rot_sin[:, rows, 0:HALF], pairs[:, :, HALF:ROT], sin_h[:, :, 0:HALF], ALU.mult)
                    dve.tensor_tensor(rot_sin[:, rows, HALF:ROT], pairs[:, :, 0:HALF], sin_h[:, :, HALF:ROT],
                                      ALU.mult).then_inc(s_rot_mul, 1)

                def residual1(g, c):
                    dve.wait_ge(s_proj, at(NG, c, g + 1))
                    dve.wait_ge(s_rinv, at(1, c, 1))
                    if g == 0 and has_f:
                        dve.wait_ge(s_x1, at(NG, f, NG))
                    for t in range(TG * g, TG * (g + 1)):
                        c = t - TG * g
                        dve.scalar_tensor_tensor(res1[:, t, :], acc[g][:, c * D:(c + 1) * D], rinv[:, t:t + 1],
                                                 xa[:, t, :], ALU.mult, ALU.add).then_inc(s_res1, 1)

                def residual2(h):
                    dve.wait_ge(s_yT, at(NG, o, h + 1))
                    if h == 0 and has_z:
                        dve.wait_ge(s_y, at(1, z, 1))
                    dve.tensor_tensor(res2[:, TG * h:TG * (h + 1), :],
                                      turn[h][:, :].rearrange("p (n d) -> p n d", d=D),
                                      x1[:, TG * h:TG * (h + 1), :], ALU.add).then_inc(s_res2, 1)

                def statistics1(h):
                    dve.wait_ge(s_res1, at(NT, f, TG * (h + 1)))
                    for t in tiles(h):
                        ins = dve.bn_stats(stat1[:, t, :], res1[:, t, :])
                    if h == NG - 1:
                        ins.then_inc(s_stat1, 1)

                def statistics2(h, c):
                    dve.wait_ge(s_res2, at(NG, c, h + 1))
                    for t in tiles(h):
                        ins = dve.bn_stats(stat2[:, t, :], res2[:, t, :])
                    if h == NG - 1:
                        ins.then_inc(s_stat2, 1)

                def normalize(dst, res, ln, t):
                    return dve.tensor_scalar(dst[:, t, :], res[:, t, :], ln[:, MEAN, t:t + 1],
                                             ln[:, RSTD, t:t + 1], ALU.subtract, ALU.mult)

                def xT_low(h):
                    low_part(xT_lo[:, halves(h)], turn[h][:, :], xT_hi[:, halves(h)], s_xT_hi, NG, q, h + 1, s_xT_lo)

                def x1T_low(h):
                    low_part(x1T_lo[:, halves(h)], turn[h][:, :], x1T_hi[:, halves(h)], s_x1T_hi, NG, f, h + 1, s_x1T_lo)

                def first_norm(h):
                    dve.wait_ge(s_ln1, at(LN_STEPS, f, LN_STEPS))
                    if has_o:
                        dve.wait_ge(s_res2, at(NG, o, h + 1))
                    for t in tiles(h):
                        ins = normalize(x1, res1, ln1, t)
                    ins.then_inc(s_x1, 1)

                def first_half_factors():
                    dve.wait_ge(s_res1, at(NT, end, TG))
                    statistics_tail(stat1, res1, 0)
                    factors(stat1, ln1, 0, 0)

                def reciprocals():
                    dve.wait_ge(s_exp, at(NT, a, NT))
                    if has_f:
                        dve.wait_ge(s_res1, at(NT, f, NT))
                    dve.reciprocal(rinv[:, :], rowsum[:, :]).then_inc(s_rinv, 1)

                def qkT_low(n):
                    h, j = n // 2, n % 2
                    low_part(qkT_lo[:, j, halves(h)], turn[j][:, :], qkT_hi[:, j, halves(h)],
                             s_qkT_hi, 2 * NG, q, n + 1, s_qkT_lo)

                def second_norm(h):
                    if h == 0:
                        dve.wait_ge(s_ln2, at(LN_STEPS, z, LN_STEPS))
                    if h == 0 and not (isinstance(b, int) and b == 3):
                        dve.wait_ge(s_stored, at(16, z, 0))
                    for t in tiles(h):
                        ins = normalize(y_out, res2, ln2, t)
                    if h == NG - 1:
                        ins.then_inc(s_y, 1)

                if isinstance(b, int) and b <= 0:
                    if has_a:
                        row_max(0)
                        row_max(1)
                        row_max(2)
                        row_max(3)
                    if setup:
                        setup_signs2()
                    if has_a:
                        row_max(4)
                    if setup:
                        setup_wvo()
                    if has_a:
                        row_max(5)
                    if setup:
                        setup_magnitudes()
                    if has_a:
                        row_max(6)
                    if setup:
                        setup_last()
                    if has_a:
                        row_max(7)
                    if has_q:
                        xT_low(0)
                        xT_low(1)
                        rotate(0)
                        rotate(1)
                    if has_a:
                        reciprocals()
                        residual1(0, a)
                        probT_copy(1, 4)
                        probT_copy(1, 5)
                        probT_copy(1, 6)
                    if early:
                        setup_signs1()
                    if has_a:
                        probT_copy(1, 7)
                    if has_q:
                        qkT_low(0)
                        qkT_low(1)
                    if early:
                        setup_wvT()
                    if has_q:
                        qkT_low(2)
                        qkT_low(3)
                    return

                if has_a:
                    row_max(0)
                if has_o:
                    hidden_high(3, o)
                if has_a:
                    row_max(1)
                if has_z:
                    statistics2(0, z)
                    statistics2(1, z)
                if has_a:
                    row_max(2)
                    row_max(3)
                    row_max(4)
                if has_z:
                    second_norm(0)
                if has_a:
                    row_max(5)
                if has_f:
                    residual1(1, f)
                    statistics1(0)
                    statistics1(1)
                if has_z:
                    second_norm(1)
                if has_a:
                    row_max(6)
                    row_max(7)
                if has_q:
                    xT_low(0)
                    xT_low(1)
                if has_o:
                    residual2(0)
                    residual2(1)
                if has_f:
                    first_norm(0)
                    first_norm(1)
                if has_q:
                    rotate(0)
                if has_a:
                    reciprocals()
                if has_f:
                    x1T_low(0)
                    x1T_low(1)
                if has_q:
                    rotate(1)
                if last:
                    statistics2(0, end2)
                if has_a:
                    residual1(0, a)
                    probT_copy(1, 4)
                    probT_copy(1, 5)
                    probT_copy(1, 6)
                    probT_copy(1, 7)
                if last:
                    first_half_factors()
                    statistics2(1, end2)
                if has_f:
                    hidden_high(0, f)
                if has_q:
                    qkT_low(0)
                    qkT_low(1)
                if has_f:
                    hidden_high(1, f)
                if has_q:
                    qkT_low(2)
                if has_f:
                    hidden_high(2, f)
                if has_q:
                    qkT_low(3)
                if last:
                    hidden_low(1, 2)

            run_steps(dve, step)

            def normalized(dst, res, ln, h):
                for t in tiles(h):
                    ins = dve.tensor_scalar(dst[:, t, :], res[:, t, :], ln[:, MEAN, t:t + 1],
                                            ln[:, RSTD, t:t + 1], ALU.subtract, ALU.mult)
                return ins

            def residual2(h, c, res2, x1):
                dve.wait_ge(s_yT, at(NG, c, h + 1))
                dve.tensor_tensor(res2[:, TG * h:TG * (h + 1), :], turn[h][:, :].rearrange("p (n d) -> p n d", d=D),
                                  x1[:, TG * h:TG * (h + 1), :], ALU.add).then_inc(s_res2, 1)

            def hidden(h, j):
                dve.wait_ge(s_gelu, at(NF, end, NF * h + j + 1))
                dve.tensor_copy(hid_hi[:, j, halves(h)], hid[:, j, halves(h)]).then_inc(s_hid_hi, 1)
                if j % 2 == 1:
                    hidden_low(j, NF * (h + 1) + j + 1, halves(h))

            def x1T_low(h):
                dve.wait_ge(s_x1T_hi, at(NG, end, h + 1))
                dve.tensor_tensor(x1T_lo[:, halves(h)], turn[h][:, :], x1T_hi[:, halves(h)].bitcast(F32),
                                  ALU.subtract).then_inc(s_x1T_lo, 1)

            def first_norm(h):
                dve.wait_ge(s_rstd, h + 1)
                normalized(x1_last, res1, ln1, h).then_inc(s_x1, 1)

            def hidden_prev():
                dve.wait_ge(s_gelu, at(NF, end1, NF))
                dve.tensor_copy(hid_hi[:, NF - 1, :], hid[:, NF - 1, :]).then_inc(s_hid_hi, 1)
                hidden_low(NF - 1, NF)

            def second_norm(h):
                if h == 0:
                    dve.wait_ge(s_ln2, at(LN_STEPS, end2, LN_STEPS))
                    dve.wait_ge(s_stored, at(16, end2, 0))
                ins = normalized(y_out, res2, ln2, h)
                if h == NG - 1:
                    ins.then_inc(s_y, 1)

            def residual1():
                dve.wait_ge(s_proj, at(NG, end, 2))
                for t in tiles(1):
                    c = t - TG
                    dve.scalar_tensor_tensor(res1[:, t, :], acc[1][:, c * D:(c + 1) * D], rinv[:, t:t + 1],
                                             xa[:, t, :], ALU.mult, ALU.add).then_inc(s_res1, 1)

            def first_factors():
                dve.wait_ge(s_res1, at(NT, end, NT))
                statistics_tail(stat1, res1, 1)
                factors(stat1, ln1, 1, 1)

            def residual2_prev(h):
                if h == 0:
                    dve.wait_ge(s_y, at(1, end2, 1))
                residual2(h, end1, res2, x1)

            def second_factors_prev():
                dve.wait_ge(s_res2, at(NG, end1, NG))
                for t in range(NT):
                    ins = dve.bn_stats(stat2[:, t, :], res2[:, t, :])
                ins.then_inc(s_stats_tail, 1)
                factors(stat2, ln2, 0, 2, NG)
                dve.tensor_scalar(ln2[:, MINUS_MEAN, :], ln2[:, MEAN, :], -1.0, None, ALU.mult).then_inc(s_minus_mean, 1)

            def residual2_last(h):
                if h == 0:
                    dve.wait_ge(s_x1, at(NG, end, NG))
                residual2(h, end, res2_last, x1_last)

            def second_factors(h):
                dve.wait_ge(s_res2, at(NG, end, h + 1))
                statistics_tail(stat1, res2_last, h)
                factors(stat1, ln1, h, 3 + h)

            def second_norm_last(h):
                dve.wait_ge(s_rstd, 4 + h)
                normalized(y_last, res2_last, ln1, h).then_inc(s_y_last, 1)

            first_norm(0)
            hidden_prev()
            second_norm(0)
            residual1()
            first_factors()
            x1T_low(0)
            second_norm(1)
            first_norm(1)
            hidden(0, 0)
            hidden(0, 1)
            hidden(0, 2)
            x1T_low(1)
            residual2_prev(0)
            hidden(0, 3)
            residual2_prev(1)
            hidden(1, 0)
            hidden(1, 1)
            hidden(1, 2)
            hidden(1, 3)
            second_factors_prev()
            residual2_last(0)
            residual2_last(1)
            second_factors(0)
            second_factors(1)
            second_norm_last(0)
            second_norm_last(1)

def rotation_tables(T, D, base=10000.0):
    P = 128
    half = D // 4
    freqs = np.power(np.float32(base), -np.arange(half, dtype=np.float32) / np.float32(half), dtype=np.float32)
    radians = np.arange(T, dtype=np.float32)[:, None] * freqs[None, :]
    cos, sin = np.cos(radians), np.sin(radians)
    tables = []
    for halves in ((cos, cos), (-sin, sin)):
        rows = np.concatenate(halves, axis=1).reshape(T // P, P, 1, 2 * half)
        tables.append(np.ascontiguousarray(np.broadcast_to(rows, (T // P, P, 2, 2 * half)).transpose(1, 0, 2, 3)))
    return tables


_INS = ['L0_attn_x', 'L0_attn_wq', 'L0_attn_wk', 'L0_attn_wv', 'L0_attn_wo',
        'L0_ffn_w1', 'L0_ffn_b1', 'L0_ffn_w2', 'L0_ffn_b2']


def kernel(**inputs):
    import concourse.bacc as _bacc
    from concourse.bass_utils import run_bass_kernel_spmd as _run

    nc = _bacc.Bacc("TRN2", target_bir_lowering=False, num_devices=1)
    given = {name: np.ascontiguousarray(inputs[name]) for name in _INS}
    given["cos"], given["sin"] = rotation_tables(given['L0_attn_x'].shape[1], given['L0_attn_x'].shape[2])
    arrays, args = {}, []
    for name, a in given.items():
        arrays[f"in_{name}_dram"] = a
        args.append(nc.dram_tensor(f"in_{name}_dram", a.shape, mybir.dt.from_np(a.dtype), kind="ExternalInput").ap())
    shape = given['L0_attn_x'].shape
    args.append(nc.dram_tensor("out_0_dram", shape, F32, kind="ExternalOutput").ap())
    attention_ffn_kernel(nc, *args)
    r = _run(nc, [arrays], core_ids=[0])
    return r.results[0]["out_0_dram"]
```
